# Optimizing a Trainium2 kernel written in Bass

```python
import numpy as np
import jax
import jax.numpy as jnp

def _softmax(x, axis=-1):
    return jax.nn.softmax(x, axis=axis)

def _gelu(x):
    return jax.nn.gelu(x, approximate=True)

def _silu(x):
    return jax.nn.silu(x)

def _sigmoid(x):
    return jax.nn.sigmoid(x)

def _layernorm(x, axis=-1, eps=1e-05):
    m = jnp.mean(x, axis=axis, keepdims=True)
    v = jnp.var(x, axis=axis, keepdims=True)
    return (x - m) / jnp.sqrt(v + eps)

def _scatter_add(tgt, idx, src, axis=0):
    return tgt.at[idx].add(src)

def _segment_sum(src, seg, n):
    return jax.ops.segment_sum(src, seg, n)
kernel_name = 'mk_adaln_d1_jaxref_r8_e40fb0'

def setup_inputs(seed: int=0):
    np.random.seed(seed)
    _w = jnp.asarray

    def _L0_attn_setup():
        import jax, jax.numpy as jnp
        import numpy as np
        INF_APPROX = 1e+30
        ROTARY_BASE = 10000.0
        D_HEAD = 128

        def _rope(x, base=ROTARY_BASE):
            _, length, _, width = x.shape
            half = width // 2
            positions = jnp.arange(length, dtype=x.dtype)
            dims = jnp.arange(half, dtype=x.dtype)
            ang_freqs = jnp.power(base, -dims / half)
            radians = positions[:, None] * ang_freqs[None, :]
            cos = jnp.cos(radians)[None, :, None, :]
            sin = jnp.sin(radians)[None, :, None, :]
            even, odd = jnp.split(x, 2, axis=-1)
            return jnp.concatenate([even * cos - odd * sin, even * sin + odd * cos], axis=-1)
        key = jax.random.key(seed)
        k1, k2, k3, k4, k5 = jax.random.split(key, 5)
        B, T, M, H, D = (2, 512, 128, 8, 128)
        n_layer = 24
        x = jax.random.normal(k1, (B, T, M), dtype=jnp.float32)
        std_qkv = M ** (-0.5)
        std_o = (M * 2 * n_layer) ** (-0.5)
        w_aq = jnp.zeros((M, H, D), dtype=jnp.float32)
        w_ak = std_qkv * jax.random.normal(k3, (M, H, D), dtype=jnp.float32)
        w_av = std_qkv * jax.random.normal(k4, (M, H, D), dtype=jnp.float32)
        w_ao = std_o * jax.random.normal(k5, (H, D, M), dtype=jnp.float32)
        return {'x': x, 'w_aq': w_aq, 'w_ak': w_ak, 'w_av': w_av, 'w_ao': w_ao}
    _L0_attn_in = _L0_attn_setup()

    def _L0_ffn_setup():
        import jax, jax.numpy as jnp
        import numpy as np
        TOP_K = 2
        NUM_EXPERTS = 8
        key = jax.random.key(seed)
        ks = jax.random.split(key, 8)
        h, d, ds, E = (128, 64, 128, NUM_EXPERTS)
        s = 1.0 / np.sqrt(h)
        return {'x': jax.random.normal(ks[0], (2, 256, h), jnp.float32), 'router': jax.random.normal(ks[1], (h, E), jnp.float32) * s, 'experts_gate': jax.random.normal(ks[2], (E, h, d), jnp.float32) * s, 'experts_up': jax.random.normal(ks[3], (E, h, d), jnp.float32) * s, 'experts_down': jax.random.normal(ks[4], (E, d, h), jnp.float32) * (1.0 / np.sqrt(d)), 'shared_gate': jax.random.normal(ks[5], (h, ds), jnp.float32) * s, 'shared_up': jax.random.normal(ks[6], (h, ds), jnp.float32) * s, 'shared_down': jax.random.normal(ks[7], (ds, h), jnp.float32) * (1.0 / np.sqrt(ds))}
    _L0_ffn_in = _L0_ffn_setup()
    _L0_c = _w((lambda *s: np.random.randn(*s).astype(np.float32) * 0.05)(2, 128))
    _L0_wmod = _w((lambda *s: np.random.randn(*s).astype(np.float32) * 0.05)(128, 6 * 128) * 128 ** (-0.5))
    _d = {'L0_attn_x': _L0_attn_in['x'], 'L0_attn_w_aq': _L0_attn_in['w_aq'], 'L0_attn_w_ak': _L0_attn_in['w_ak'], 'L0_attn_w_av': _L0_attn_in['w_av'], 'L0_attn_w_ao': _L0_attn_in['w_ao'], 'L0_ffn_router': _L0_ffn_in['router'], 'L0_ffn_experts_gate': _L0_ffn_in['experts_gate'], 'L0_ffn_experts_up': _L0_ffn_in['experts_up'], 'L0_ffn_experts_down': _L0_ffn_in['experts_down'], 'L0_ffn_shared_gate': _L0_ffn_in['shared_gate'], 'L0_ffn_shared_up': _L0_ffn_in['shared_up'], 'L0_ffn_shared_down': _L0_ffn_in['shared_down'], 'L0_c': _L0_c, 'L0_wmod': _L0_wmod}
    _x0 = _d['L0_attn_x']
    _d['L0_attn_x'] = jax.random.normal(jax.random.fold_in(jax.random.key(seed), 1), (2, 1024, 128), dtype=_x0.dtype)
    del _x0
    return _d

def reference(L0_attn_x, L0_attn_w_aq, L0_attn_w_ak, L0_attn_w_av, L0_attn_w_ao, L0_ffn_router, L0_ffn_experts_gate, L0_ffn_experts_up, L0_ffn_experts_down, L0_ffn_shared_gate, L0_ffn_shared_up, L0_ffn_shared_down, L0_c, L0_wmod):

    def _L0_attn_ref(x, w_aq, w_ak, w_av, w_ao):
        import jax, jax.numpy as jnp
        import numpy as np
        INF_APPROX = 1e+30
        ROTARY_BASE = 10000.0
        D_HEAD = 128

        def _rope(x, base=ROTARY_BASE):
            _, length, _, width = x.shape
            half = width // 2
            positions = jnp.arange(length, dtype=x.dtype)
            dims = jnp.arange(half, dtype=x.dtype)
            ang_freqs = jnp.power(base, -dims / half)
            radians = positions[:, None] * ang_freqs[None, :]
            cos = jnp.cos(radians)[None, :, None, :]
            sin = jnp.sin(radians)[None, :, None, :]
            even, odd = jnp.split(x, 2, axis=-1)
            return jnp.concatenate([even * cos - odd * sin, even * sin + odd * cos], axis=-1)
        B, T, M = x.shape
        q = jnp.einsum('btm,mhd->bthd', x, w_aq)
        k = jnp.einsum('btm,mhd->bthd', x, w_ak)
        v = jnp.einsum('btm,mhd->bthd', x, w_av)
        q = _rope(q)
        k = _rope(k)
        s = jnp.einsum('bihd,bjhd->bhij', q, k) / D_HEAD
        i = jnp.arange(T)[:, None]
        j = jnp.arange(T)[None, :]
        mask = (i < j).astype(x.dtype)[None, None, :, :]
        s = s - jnp.asarray(INF_APPROX, x.dtype) * mask
        p = jax.nn.softmax(s, axis=-1)
        o = jnp.einsum('bhij,bjhd->bihd', p, v)
        r = jnp.einsum('bihd,hdm->bim', o, w_ao)
        return r

    def _L0_ffn_ref(x, router, experts_gate, experts_up, experts_down, shared_gate, shared_up, shared_down):
        import jax, jax.numpy as jnp
        import numpy as np
        TOP_K = 2
        NUM_EXPERTS = 8
        b, s, h = x.shape
        E = router.shape[1]
        shared_act = jax.nn.silu(jnp.einsum('bsh,hd->bsd', x, shared_gate))
        shared_up_out = jnp.einsum('bsh,hd->bsd', x, shared_up)
        shared_out = jnp.einsum('bsd,dh->bsh', shared_act * shared_up_out, shared_down)
        router_probs = jax.nn.softmax(jnp.einsum('bsh,he->bse', x, router), axis=-1)
        topk_probs, topk_idx = jax.lax.top_k(router_probs, TOP_K)
        coef = jnp.sum(jax.nn.one_hot(topk_idx, E, dtype=x.dtype) * topk_probs[..., None], axis=2)
        coef = coef.reshape(b * s, E)
        x_flat = x.reshape(b * s, h)
        gate = jnp.einsum('th,ehd->etd', x_flat, experts_gate)
        up = jnp.einsum('th,ehd->etd', x_flat, experts_up)
        expert_out = jnp.einsum('etd,edh->eth', jax.nn.silu(gate) * up, experts_down)
        routed = jnp.einsum('eth,te->th', expert_out, coef)
        return routed.reshape(b, s, h) + shared_out
    x = L0_attn_x
    mod = (_silu(L0_c) @ L0_wmod).reshape(L0_c.shape[0], 6, 1, -1)
    sa, ca, ga, sb, cb, gb = (mod[:, 0], mod[:, 1], mod[:, 2], mod[:, 3], mod[:, 4], mod[:, 5])
    ga = (2 * (ga >= 0) - 1) * jnp.maximum(jnp.abs(ga), 0.25)
    gb = (2 * (gb >= 0) - 1) * jnp.maximum(jnp.abs(gb), 0.25)
    h = _layernorm(x, axis=-1) * (1 + ca) + sa
    x = x + ga * _L0_attn_ref(h, L0_attn_w_aq, L0_attn_w_ak, L0_attn_w_av, L0_attn_w_ao)
    h = _layernorm(x, axis=-1) * (1 + cb) + sb
    x = x + gb * _L0_ffn_ref(h, L0_ffn_router, L0_ffn_experts_gate, L0_ffn_experts_up, L0_ffn_experts_down, L0_ffn_shared_gate, L0_ffn_shared_up, L0_ffn_shared_down)
    return x

_drawn_inputs = setup_inputs


def setup_inputs(seed=0):
    import zlib

    import numpy as np

    out = dict(_drawn_inputs(seed))
    spreads = {'L0_attn_w_aq': (0.0, 0.8)}
    factors = {'L0_attn_w_ak': 8.0,
     'L0_attn_w_av': 6.438,
     'L0_attn_w_ao': 6.434,
     'L0_ffn_router': 3.153,
     'L0_ffn_experts_gate': 3.01,
     'L0_ffn_experts_up': 2.821,
     'L0_ffn_experts_down': 2.83}
    for name, (base, spread) in spreads.items():
        noise = np.random.default_rng([zlib.crc32(name.encode()), seed]).standard_normal(out[name].shape)
        drawn = base * np.exp(spread * noise) if base else spread * noise
        out[name] = jnp.asarray(drawn.astype(out[name].dtype))
    for name, factor in factors.items():
        out[name] = (out[name] * factor).astype(out[name].dtype)
    return out
```

```python
from contextlib import ExitStack

import numpy as np

import concourse.bass as bass
from concourse import mybir

F32 = mybir.dt.float32
F32R = mybir.dt.float32r
BF16 = mybir.dt.bfloat16
ALU = mybir.AluOpType
ACT = mybir.ActivationFunctionType
AX = mybir.AxisListType

P = 128
RING = 3
EPS = 1e-5
ROUTE = 14
BLOCK = 512
TPB = BLOCK // P
SHIFT, SCALE, GATE = 0, 1, 2


STAGE = """
T' 5 0; A' 0 0 1; S 0; I' 7; N' 7; T' 5 1; X 0; A' 0 1 2
T' 6 0; A' 0 2 4; S 1; I 0; N 0; T' 6 1; X 1
T' 7 0; S 2; I 1; N 1; O' 0; T' 7 1; X 2
R 1 0; S 3; I 2; N 2; R 1 1; A' 1 0 2; T 0 0; X 3; A' 1 2 3; P+ 0; P+ 1
S 4; I 3; N 3; T 1 0; A' 1 3 4; P+ 2; X 4; A' 1 4 5; P+ 3
S 5; I 4; N 4; T 2 0; A' 1 5 6; P+ 4; X 5; A' 1 6 7; P+ 5
S 6; I 5; N 5; T 3 0; A' 1 7 8; X 6; P+ 6
R+ 0 0; S 7; I 6; N 6; R+ 0 1; T 4 0; O' 1; X 7; T 4 1; P+ 7
"""
FIRST = "P+ 0; P+ 1; P+ 2; P+ 3; P+ 4; R+ 0 0; P+ 5; R+ 0 1; P+ 6; P+ 7"
LAST = """T' 5 0; I' 7; N' 7; A' 0 0 1; T' 5 1; A' 0 1 2; T' 6 0; A' 0 2 4; T' 6 1; T' 7 0; O' 0; T' 7 1; A' 1 0 8; O' 1"""
RING_STEPS = ("T", "P", "R")


def steps(text, n, heads):
    for step in text.replace("\n", ";").split(";"):
        if step.strip():
            name, *tiles = step.split()
            head = n + {"'": -1, "+": 1}.get(name[1:], 0)
            if 0 <= head < heads:
                yield (name[0], head, *map(int, tiles))


def ring_plan(heads):
    every = [s for n in range(-1, heads + 1)
             for s in steps(FIRST if n < 0 else LAST if n == heads else STAGE, n, heads)]
    return {s: i for i, s in enumerate(s for s in every if s[0] in RING_STEPS)}


def build(nc, x, w_qk, w_vT, w_o, router, w_gate_up, w_down, cT, w_mod, cos_t, sin_t, causal, ident_in, out):
    B, T, M = x.shape
    H = w_qk.shape[1]
    D = w_qk.shape[2] // 2
    E = router.shape[1]
    TILES = T // P
    NBLK = T // BLOCK
    HALF = D // 2
    QKV = 3 * D
    PAIRS = w_down.shape[1]
    EPAIRS = E // 2
    SM = 1.0 / D
    assert (M, D, TILES, NBLK) == (P, P, 8, 2)
    LOOPED = (H - 2) // 2
    RI = ring_plan(H)
    RB = len(RI)
    OUTS = NBLK * H + 1
    PER = (RI[("T", 3, 0, 0)] - RI[("T", 1, 0, 0)])
    assert PER % RING == 0 and RB % RING == 0

    with ExitStack() as ctx:
        def sb(name, shape, dt=F32):
            return ctx.enter_context(nc.sbuf_tensor(name, shape, dt))

        def sem(name):
            return ctx.enter_context(nc.semaphore(name))

        ps = ctx.enter_context(nc.psum_tensor("ps", [P, 8, BLOCK], F32))
        OUT_BANK, RING0 = 4, 5

        wqkv = [sb(f"wqkv_{s}", [P, H, QKV], F32R) for s in ("hi", "lo")]
        wgu = [sb(f"wgu_{s}", [P, 2 * PAIRS, P], F32R) for s in ("hi", "lo")]
        wdn = [sb(f"wdn_{s}", [P, PAIRS, P], F32R) for s in ("hi", "lo")]
        router_sb = sb("router_sb", [P, E])
        cos_sb = sb("cos_sb", [P, TILES, HALF])
        sin_sb = sb("sin_sb", [P, TILES, D])
        ident = sb("ident", [P, P])
        identb = sb("identb", [P, P], BF16)
        causalb = sb("causalb", [P, P], BF16)
        c_sb = sb("c_sb", [P, B])
        csilu = sb("csilu", [P, B])
        mod_all = sb("mod_all", [P, 6, B])
        mod_sign = sb("mod_sign", [P, 2, B])
        mod_size = sb("mod_size", [P, 2, B])
        mod = sb("mod", [P, 6])
        x_in = sb("x_in", [P, TILES, M])
        x_mid = sb("x_mid", [P, TILES, M])
        stats = sb("stats", [P, TILES, 6])
        mean_sum = sb("mean_sum", [P, TILES])
        mean_gap = sb("mean_gap", [P, TILES])
        mean = sb("mean", [P, TILES])
        gap2 = sb("gap2", [P, TILES])
        squares = sb("squares", [P, TILES])
        squares2 = sb("squares2", [P, TILES])
        vareps = sb("vareps", [P, TILES])
        minus_half = sb("minus_half", [P, TILES])
        rstd = sb("rstd", [P, TILES])
        normed = sb("normed", [P, TILES, M])
        hT = sb("hT", [P, T])
        hT_hl = [sb(f"hT_{s}", [P, T], F32R) for s in ("hi", "lo")]
        q_hl = [[sb(f"q_{s}{k}", [P, T], F32R) for s in ("hi", "lo")] for k in range(2)]
        k_hl = [[sb(f"k_{s}{k}", [P, T], F32R) for s in ("hi", "lo")] for k in range(2)]
        v_hl = [[sb(f"v_{s}{k}", [P, TILES, M], F32R) for s in ("hi", "lo")] for k in range(2)]
        qk_raw = sb("qk_raw", [P, 2, 2 * D])
        cos_part = sb("cos_part", [P, 2, 2 * D])
        sin_part = sb("sin_part", [P, 2, 2 * D])
        rotated = sb("rotated", [P, TILES, 2 * D])
        probs = sb("probs", [P, 4, T])
        probsT = [[sb(f"probsT{k}_{s}", [P, TPB * (k + 1), BLOCK], F32R) for s in ("hi", "lo")] for k in range(NBLK)]
        neg_max = sb("neg_max", [P, TILES])
        row_sum = sb("row_sum", [P, TILES])
        inv_sum = sb("inv_sum", [P, TILES])
        attnT = sb("attnT", [P, T])
        lmax = sb("lmax", [P, TILES])
        lsub = sb("lsub", [P, TILES, E])
        lexp = sb("lexp", [P, TILES, E])
        lsum = sb("lsum", [P, TILES])
        linv = sb("linv", [P, TILES])
        rprob = sb("rprob", [P, TILES, E])
        rank = sb("rank", [P, TILES, E])
        top = sb("top", [P, 2, TILES])
        tie = sb("tie", [P, 2, TILES, E])
        first = sb("first", [P, 2, TILES])
        chosen = sb("chosen", [P, 2, TILES, E])
        rest = sb("rest", [P, TILES, E])
        coef = sb("coef", [P, TILES, E])
        out_sb = sb("out_sb", [P, TILES, M])

        st_qk = probs[:, 0:2, :].rearrange("p a (h d) -> p (a h) d", d=2 * D)
        st_vT = probs[:, 2, :].rearrange("p (h d) -> p h d", d=D)
        st_o = probs[:, 3, :].rearrange("p (h d) -> p h d", d=M)
        st_gu = rotated[:, 0:TILES, :].rearrange("p a d -> p (a d)")[:, 0:2 * PAIRS * P].rearrange("p (g d) -> p g d", d=P)
        st_dn = x_mid[:, 0:PAIRS, :].rearrange("p a d -> p (a d)").rearrange("p (g d) -> p g d", d=P)
        st_mod = normed[:, 0:6, :]
        causal_f = normed[:, 6, :]
        def silu_buf(i):
            return probs[:, 0, (i % 2) * BLOCK:(i % 2 + 1) * BLOCK]

        def gated_buf(i):
            return probs[:, 1, (i % 2) * BLOCK:(i % 2 + 1) * BLOCK]

        def act_buf(i):
            return probs[:, 2, (i % 2) * BLOCK:(i % 2 + 1) * BLOCK]

        def act_hl(s, i):
            return probsT[1][s][:, i, :]

        def coef_buf(i):
            return rotated[:, 2 * (i % 4):2 * (i % 4) + 2, :].rearrange("p a (t d) -> p (a t) d", d=P)

        yT = probs[:, 3, :]

        x_loaded = sem("x_loaded")
        qk_loaded = sem("qk_loaded")
        vo_loaded = sem("vo_loaded")
        mod_loaded = sem("mod_loaded")
        tables_loaded = sem("tables_loaded")
        ffn_loaded = sem("ffn_loaded")
        consts_ready = sem("consts_ready")
        c_ready = sem("c_ready")
        mod_filled = sem("mod_filled")
        mod_steps = sem("mod_steps")
        wqk_hi_ready = sem("wqk_hi_ready")
        wqk_ready = sem("wqk_ready")
        wvo_filled = sem("wvo_filled")
        wvo_hi_ready = sem("wvo_hi_ready")
        wvo_ready = sem("wvo_ready")
        wffn_hi_ready = sem("wffn_hi_ready")
        wffn_ready = sem("wffn_ready")
        mod_picked = sem("mod_picked")
        stats_ready = sem("stats_ready")
        halves_ready = sem("halves_ready")
        var_steps = sem("var_steps")
        pool_waits = sem("pool_waits")
        vareps_ready = sem("vareps_ready")
        rstd_ready = sem("rstd_ready")
        normed_ready = sem("normed_ready")
        normedT_filled = sem("normedT_filled")
        hT_ready = sem("hT_ready")
        hT_hi_ready = sem("hT_hi_ready")
        hT_lo_ready = sem("hT_lo_ready")
        ring_filled = sem("ring_filled")
        ring_hi_ready = sem("ring_hi_ready")
        ring_done = sem("ring_done")
        sin_ready = sem("sin_ready")
        rotated_ready = sem("rotated_ready")
        scores_filled = sem("scores_filled")
        max_ready = sem("max_ready")
        exp_ready = sem("exp_ready")
        inv_ready = sem("inv_ready")
        probs_ready = sem("probs_ready")
        outT_filled = sem("outT_filled")
        outT_added = sem("outT_added")
        attn_gated = sem("attn_gated")
        attn_filled = sem("attn_filled")
        x_mid_ready = sem("x_mid_ready")
        logits_filled = sem("logits_filled")
        route_steps = sem("route_steps")
        route_exp = sem("route_exp")
        tie_ready = sem("tie_ready")
        coef_spread = sem("coef_spread")
        gate_filled = sem("gate_filled")
        up_filled = sem("up_filled")
        coefT_filled = sem("coefT_filled")
        silu_ready = sem("silu_ready")
        gated_ready = sem("gated_ready")
        act_ready = sem("act_ready")
        act_hi_ready = sem("act_hi_ready")
        act_lo_ready = sem("act_lo_ready")
        y_filled = sem("y_filled")
        yT_ready = sem("yT_ready")
        y_turned = sem("y_turned")
        out_ready = sem("out_ready")
        stored = sem("stored")

        def pos(b, p, count, per_batch, per_pair=0):
            v = b * per_batch + count
            return v if p is None else v + p * per_pair

        def by_head(n, t):
            return TILES * n + t + 1

        def wait_tile(eng, s, b, p, n, t):
            eng.wait_ge(s, pos(b, p, by_head(n, t), TILES * H, 2 * TILES))

        def wait_ring(eng, s, b, p, unit, back=0):
            eng.wait_ge(s, pos(b, p, RI[unit] + 1 - back, RB, PER))

        def bank_of(unit):
            return RING0 + RI[unit] % RING

        def score_cols(t):
            w = (t + 1) * P
            if w == BLOCK + P:
                return P, [(P, 0, 3 * P), (BLOCK, 3 * P, 2 * P)]
            return 0, [(c, c, min(BLOCK, w - c)) for c in range(0, w, BLOCK)]

        def score_pair(t):
            return ps[:, 2 * (t % 2):2 * (t % 2) + 2, :].rearrange("p a c -> p (a c)")

        def view(ap, dims, offset=0):
            return bass.AP(ap.tensor, ap.offset + offset, [ap.ap[0]] + dims)

        block = ctx.enter_context(nc.Block())

        @block.sync
        def _(sp):
            sp.dma_start(c_sb[:], cT).then_inc(mod_loaded, 16)
            sp.dma_start(st_mod, w_mod).then_inc(mod_loaded, 16)
            sp.dma_start(ident[:], ident_in).then_inc(tables_loaded, 16)
            sp.dma_start(causal_f, causal).then_inc(tables_loaded, 16)
            sp.dma_start(st_qk, w_qk).then_inc(qk_loaded, 16)
            sp.dma_start(cos_sb[:], cos_t).then_inc(tables_loaded, 16)
            sp.dma_start(sin_sb[:], sin_t).then_inc(tables_loaded, 16)
            sp.sem_inc(x_mid_ready, 1)
            sp.sem_inc(stored, 16)
            with sp.Fori(0, B) as b:
                sp.wait_ge(x_mid_ready, b * NBLK + 1)
                sp.dma_start(x_in[:], x[b].rearrange("(t p) m -> p t m", p=P)).then_inc(x_loaded, 16)
                for k in range(NBLK):
                    sp.wait_ge(out_ready, b * NBLK + k + 1)
                    sp.dma_start(out[b].rearrange("(k t p) m -> k p t m", p=P, t=TPB)[k],
                                 out_sb[:, TPB * k:TPB * (k + 1), :]).then_inc(stored, 16)
            sp.wait_ge(stored, 16 * B * NBLK + 16)

        @block.gpsimd
        def _(pool):
            pool.dma_start(st_vT, w_vT).then_inc(vo_loaded, 16)
            pool.dma_start(st_o, w_o).then_inc(vo_loaded, 16)
            pool.dma_start(st_gu, w_gate_up).then_inc(ffn_loaded, 16)
            pool.dma_start(st_dn, w_down).then_inc(ffn_loaded, 16)
            pool.dma_start(router_sb[:], router).then_inc(ffn_loaded, 16)
            pool.memset(minus_half[:], -0.5)
            for e in range(E):
                ins = pool.memset(rank[:, :, e], float(E - e))
            ins.then_inc(consts_ready, 1)
            pool.wait_ge(ffn_loaded, 48)
            pool.tensor_scalar(wgu[0][:], st_gu, 1.0, 1.0, ALU.mult, ALU.mult)
            pool.tensor_scalar(wdn[0][:], st_dn, 1.0, 1.0, ALU.mult, ALU.mult).then_inc(wffn_hi_ready, 1)
            pool.wait_ge(wffn_hi_ready, 1)
            pool.tensor_tensor(wgu[1][:], st_gu, wgu[0][:].bitcast(F32), ALU.subtract)
            pool.tensor_tensor(wdn[1][:], st_dn, wdn[0][:].bitcast(F32), ALU.subtract).then_inc(wffn_ready, 1)
            pool.wait_ge(consts_ready, 1)

            def rstd_step(i, b):
                k = 2 * b + i + 1
                pool.wait_ge(vareps_ready, k)
                pool.tensor_tensor(rstd[:], vareps[:], minus_half[:], ALU.pow).then_inc(rstd_ready, 1)

            def rotate(b, p, n, t):
                unit = ("P", n, t)
                raw = qk_raw[:, t % 2, :]
                swapped = view(raw, [[D, 2], [-HALF, 2], [1, HALF]], HALF)
                wait_ring(pool, ring_hi_ready, b, p, unit)
                pool.tensor_tensor(view(sin_part[:, t % 2, :], [[D, 2], [HALF, 2], [1, HALF]]), swapped,
                                   view(sin_sb[:, t, :], [[0, 2], [HALF, 2], [1, HALF]]), ALU.mult).then_inc(sin_ready, 1)
                wait_tile(pool, sin_ready, b, p, n, t)
                wait_ring(pool, ring_done, b, p, unit)
                pool.tensor_tensor(rotated[:, t, :], cos_part[:, t % 2, :], sin_part[:, t % 2, :],
                                   ALU.add).then_inc(rotated_ready, 1)

            def normalise(b, p, n, t):
                w = (t + 1) * P
                wait_tile(pool, inv_ready, b, p, n, t)
                pool.sem_inc(pool_waits, 1)
                pool.tensor_scalar(probs[:, t % 4, 0:w], probs[:, t % 4, 0:w], inv_sum[:, t:t + 1], 1.0,
                                   ALU.mult, ALU.mult).then_inc(probs_ready, 1)

            def walk(b, p, text, n):
                for name, head, t, *_ in steps(text, n, H):
                    if name == "N":
                        normalise(b, p, head, t)
                    elif name == "P":
                        rotate(b, p, head, t)

            with pool.Fori(0, B) as b:
                rstd_step(0, b)
                walk(b, None, FIRST, -1)
                walk(b, None, STAGE, 0)
                with pool.Fori(0, LOOPED) as p:
                    walk(b, p, STAGE, 1)
                    walk(b, p, STAGE, 2)
                walk(b, None, STAGE, H - 1)
                walk(b, None, LAST, H)
                rstd_step(1, b)
                pool.wait_ge(route_steps, pos(b, None, ROUTE, ROUTE))
                pool.sem_inc(pool_waits, 1)
                for k in range(NBLK):
                    for g in range(EPAIRS):
                        i = EPAIRS * k + g
                        if i >= 4:
                            pool.wait_ge(coefT_filled, pos(b, None, i - 3, NBLK * EPAIRS))
                            pool.sem_inc(pool_waits, 1)
                        pool.tensor_scalar(coef_buf(i).rearrange("p t (e d) -> p t e d", e=2),
                                           view(coef[:, TPB * k, 2 * g:2 * g + 2], [[E, TPB], [1, 2], [0, P // 2]]),
                                           1.0, 1.0, ALU.mult, ALU.mult).then_inc(coef_spread, 1)

        @block.scalar
        def _(act):
            act.wait_ge(mod_loaded, 32)
            act.activation(csilu[:], c_sb[:], ACT.Silu).then_inc(c_ready, 1)
            act.wait_ge(tables_loaded, 64)
            act.copy(identb[:], ident[:])
            act.copy(causalb[:], causal_f).then_inc(consts_ready, 1)
            act.wait_ge(qk_loaded, 16)
            act.copy(wqkv[0][:, :, 0:2 * D], st_qk).then_inc(wqk_hi_ready, 1)
            act.wait_ge(wvo_filled, 1)
            act.copy(wqkv[0][:, :, 2 * D:QKV], ps[:, 0:2, :].rearrange("p a (h m) -> p (a h) m", m=M)).then_inc(wvo_hi_ready, 1)

            def modulate(i, b):
                for k in range(NBLK):
                    cols = slice(BLOCK * k, BLOCK * (k + 1))
                    c = pos(b, None, NBLK * i + k + 1, 2 * NBLK)
                    act.wait_ge(normedT_filled, c)
                    act.activation(hT[:, cols], ps[:, 2 + k, :], ACT.Identity, bias=mod[:, 3 * i + SHIFT:3 * i + SHIFT + 1],
                                   scale=mod[:, 3 * i + SCALE:3 * i + SCALE + 1]).then_inc(hT_ready, 1)
                    act.wait_ge(hT_ready, c)
                    act.copy(hT_hl[0][:, cols], hT[:, cols]).then_inc(hT_hi_ready, 1)

            def exponent(b, p, n, t):
                at, _ = score_cols(t)
                w = (t + 1) * P
                wait_tile(act, max_ready, b, p, n, t)
                act.activation(probs[:, t % 4, 0:w], score_pair(t)[:, at:at + w], ACT.Exp, bias=neg_max[:, t:t + 1],
                               accum_out=row_sum[:, t:t + 1]).then_inc(exp_ready, 1)

            def take_hi(b, p, unit):
                kind, n, t = unit[:3]
                bank = ps[:, bank_of(unit), :]
                if kind == "P":
                    if (n, t) >= (0, 2):
                        m = (n, t - 2) if t >= 2 else (n - 1, t + TILES - 2)
                        wait_tile(act, sin_ready, b, p, *m)
                    wait_ring(act, ring_filled, b, p, unit)
                    act.copy(qk_raw[:, t % 2, :], bank[:, 0:2 * D])
                    act.copy(v_hl[n % 2][0][:, t, :], bank[:, 2 * D:QKV]).then_inc(ring_hi_ready, 1)
                elif kind == "R":
                    dst = (q_hl, k_hl)[unit[3]][n % 2][0][:, BLOCK * t:BLOCK * (t + 1)]
                    wait_ring(act, ring_filled, b, p, unit)
                    act.activation(dst, bank, ACT.Copy, scale=(SM, 1.0)[unit[3]]).then_inc(ring_hi_ready, 1)
                else:
                    j0 = TPB * unit[3]
                    k = min(TPB, t + 1 - j0)
                    wait_ring(act, ring_filled, b, p, unit)
                    act.copy(probsT[t // TPB][0][:, j0:j0 + k, P * (t % TPB):P * (t % TPB + 1)],
                             bank[:, 0:k * P].rearrange("p (j i) -> p j i", i=P)).then_inc(ring_hi_ready, 1)

            def walk(b, p, text, n):
                for step in steps(text, n, H):
                    if step[0] == "X":
                        exponent(b, p, *step[1:])
                    elif step[0] in RING_STEPS:
                        take_hi(b, p, step)

            with act.Fori(0, B) as b:
                act.wait_ge(mod_picked, b + 1)
                modulate(0, b)
                walk(b, None, FIRST, -1)
                walk(b, None, STAGE, 0)
                with act.Fori(0, LOOPED) as p:
                    walk(b, p, STAGE, 1)
                    walk(b, p, STAGE, 2)
                walk(b, None, STAGE, H - 1)
                walk(b, None, LAST, H)
                modulate(1, b)
                act.wait_ge(route_steps, pos(b, None, 2, ROUTE))
                act.activation(lexp[:], lsub[:], ACT.Exp).then_inc(route_exp, 1)
                for k in range(NBLK):
                    for g in range(PAIRS):
                        i = PAIRS * k + g
                        c = pos(b, None, i + 1, NBLK * PAIRS)
                        act.wait_ge(gate_filled, c)
                        if i >= 2:
                            act.wait_ge(gated_ready, c - 2)
                        act.activation(silu_buf(i), ps[:, i % 2, :], ACT.Silu).then_inc(silu_ready, 1)
                        act.wait_ge(act_ready, c)
                        act.copy(act_hl(0, g), act_buf(i)).then_inc(act_hi_ready, 1)
                    act.wait_ge(y_filled, pos(b, None, k + 1, NBLK))
                    act.activation(yT[:, BLOCK * k:BLOCK * (k + 1)], ps[:, 4, :], ACT.Copy,
                                   scale=mod[:, 3 + GATE:3 + GATE + 1]).then_inc(yT_ready, 1)

        @block.vector
        def _(dve):
            dve.wait_ge(mod_filled, 1)
            dve.tensor_copy(mod_all[:], ps[:, 7, 0:6 * B].rearrange("p (k b) -> p k b", b=B)).then_inc(mod_steps, 1)
            dve.wait_ge(mod_steps, 1)
            scales = view(mod_all[:], [[3 * B, 2], [1, B]], SCALE * B)
            gates = view(mod_all[:], [[3 * B, 2], [1, B]], GATE * B)
            dve.tensor_scalar(scales, scales, 1.0, None, ALU.add).then_inc(mod_steps, 1)
            dve.tensor_scalar(mod_sign[:], gates, 0.0, 2.0, ALU.is_ge, ALU.mult).then_inc(mod_steps, 1)
            dve.scalar_tensor_tensor(mod_size[:], gates, -1.0, gates, ALU.mult, ALU.max).then_inc(mod_steps, 1)
            dve.wait_ge(mod_steps, 4)
            dve.tensor_scalar(mod_sign[:], mod_sign[:], -1.0, None, ALU.add).then_inc(mod_steps, 1)
            dve.wait_ge(mod_steps, 5)
            dve.scalar_tensor_tensor(gates, mod_size[:], 0.25, mod_sign[:], ALU.max, ALU.mult).then_inc(mod_steps, 1)
            dve.wait_ge(wqk_hi_ready, 1)
            dve.tensor_tensor(wqkv[1][:, :, 0:2 * D], st_qk, wqkv[0][:, :, 0:2 * D].bitcast(F32),
                              ALU.subtract).then_inc(wqk_ready, 1)
            dve.wait_ge(wvo_hi_ready, 1)
            dve.tensor_tensor(wqkv[1][:, :, 2 * D:QKV], ps[:, 0:2, :].rearrange("p a (h m) -> p (a h) m", m=M),
                              wqkv[0][:, :, 2 * D:QKV].bitcast(F32), ALU.subtract).then_inc(wvo_ready, 1)
            dve.wait_ge(mod_steps, 6)

            def normalise_rows(i, b, src):
                k = 2 * b + i + 1
                for t in range(TILES):
                    ins = dve.bn_stats(stats[:, t, :], src[:, t, :])
                ins.then_inc(stats_ready, 1)
                dve.wait_ge(stats_ready, k)
                dve.tensor_tensor(mean_sum[:], stats[:, :, 1], stats[:, :, 4], ALU.add)
                dve.tensor_tensor(mean_gap[:], stats[:, :, 1], stats[:, :, 4], ALU.subtract)
                dve.tensor_tensor(squares[:], stats[:, :, 2], stats[:, :, 5], ALU.add).then_inc(halves_ready, 1)
                dve.wait_ge(halves_ready, k)
                dve.tensor_scalar(mean[:], mean_sum[:], 0.5, None, ALU.mult)
                dve.scalar_tensor_tensor(gap2[:], mean_gap[:], 0.25, mean_gap[:], ALU.mult, ALU.mult)
                dve.tensor_scalar(squares2[:], squares[:], 1.0 / M, EPS, ALU.mult, ALU.add).then_inc(var_steps, 1)
                dve.wait_ge(var_steps, k)
                dve.tensor_tensor(vareps[:], gap2[:], squares2[:], ALU.add).then_inc(vareps_ready, 1)
                dve.wait_ge(rstd_ready, k)
                for t in range(TILES):
                    dve.tensor_scalar(normed[:, t, :], src[:, t, :], mean[:, t:t + 1], rstd[:, t:t + 1],
                                      ALU.subtract, ALU.mult).then_inc(normed_ready, 1)

            def hT_lo(i, b):
                for k in range(NBLK):
                    cols = slice(BLOCK * k, BLOCK * (k + 1))
                    dve.wait_ge(hT_hi_ready, pos(b, None, NBLK * i + k + 1, 2 * NBLK))
                    dve.tensor_tensor(hT_hl[1][:, cols], hT[:, cols], hT_hl[0][:, cols].bitcast(F32),
                                      ALU.subtract).then_inc(hT_lo_ready, 1)

            def row_max(b, p, n, t):
                at, _ = score_cols(t)
                wait_tile(dve, scores_filled, b, p, n, t)
                dve.tensor_reduce(neg_max[:, t:t + 1], score_pair(t)[:, at:at + (t + 1) * P], AX.X, ALU.max,
                                  negate=True).then_inc(max_ready, 1)

            def invert(b, p, n, t):
                wait_tile(dve, exp_ready, b, p, n, t)
                dve.reciprocal(inv_sum[:, t:t + 1], row_sum[:, t:t + 1]).then_inc(inv_ready, 1)

            def take_lo(b, p, unit):
                kind, n, t = unit[:3]
                bank = ps[:, bank_of(unit), :]
                if kind == "P":
                    if (n, t) >= (0, 2):
                        m = (n, t - 2) if t >= 2 else (n - 1, t + TILES - 2)
                        wait_tile(dve, rotated_ready, b, p, *m)
                    wait_ring(dve, ring_hi_ready, b, p, unit)
                    dve.tensor_tensor(view(cos_part[:, t % 2, :], [[HALF, 4], [1, HALF]]), view(bank, [[HALF, 4], [1, HALF]]),
                                      view(cos_sb[:, t, :], [[0, 4], [1, HALF]]), ALU.mult)
                    dve.tensor_tensor(v_hl[n % 2][1][:, t, :], bank[:, 2 * D:QKV], v_hl[n % 2][0][:, t, :].bitcast(F32),
                                      ALU.subtract).then_inc(ring_done, 1)
                elif kind == "R":
                    hi, lo = ((q_hl, k_hl)[unit[3]][n % 2][s][:, BLOCK * t:BLOCK * (t + 1)] for s in (0, 1))
                    wait_ring(dve, ring_hi_ready, b, p, unit)
                    dve.scalar_tensor_tensor(lo, bank, (SM, 1.0)[unit[3]], hi.bitcast(F32), ALU.mult,
                                             ALU.subtract).then_inc(ring_done, 1)
                else:
                    j0 = TPB * unit[3]
                    k = min(TPB, t + 1 - j0)
                    hi, lo = (probsT[t // TPB][s][:, j0:j0 + k, P * (t % TPB):P * (t % TPB + 1)] for s in (0, 1))
                    wait_ring(dve, ring_hi_ready, b, p, unit)
                    dve.tensor_tensor(lo, bank[:, 0:k * P].rearrange("p (j i) -> p j i", i=P), hi.bitcast(F32),
                                      ALU.subtract).then_inc(ring_done, 1)

            def add_out(b, p, n, k):
                part = attnT[:, BLOCK * k:BLOCK * (k + 1)]
                dve.wait_ge(outT_filled, pos(b, p, NBLK * n + k + 1, NBLK * H, 2 * NBLK))
                dve.tensor_tensor(part, part, ps[:, OUT_BANK, :], ALU.add).then_inc(outT_added, 1)

            def walk(b, p, text, n):
                for step in steps(text, n, H):
                    if step[0] == "S":
                        row_max(b, p, *step[1:])
                    elif step[0] == "I":
                        invert(b, p, *step[1:])
                    elif step[0] == "O":
                        add_out(b, p, *step[1:])
                    elif step[0] in RING_STEPS:
                        take_lo(b, p, step)

            def route(b):
                done = [0]

                def step(ins):
                    done[0] += 1
                    ins.then_inc(route_steps, 1)

                def after(n):
                    dve.wait_ge(route_steps, pos(b, None, n, ROUTE))

                logits = ps[:, 7, 0:TILES * E].rearrange("p (t e) -> p t e", e=E)

                def spread(a):
                    return view(a, [[1, TILES], [0, E]])

                dve.wait_ge(logits_filled, b + 1)
                step(dve.tensor_reduce(lmax[:], logits, AX.X, ALU.max))
                after(1)
                step(dve.tensor_tensor(lsub[:], logits, spread(lmax[:]), ALU.subtract))
                dve.wait_ge(route_exp, b + 1)
                step(dve.tensor_reduce(lsum[:], lexp[:], AX.X, ALU.add))
                after(3)
                step(dve.reciprocal(linv[:], lsum[:]))
                after(4)
                step(dve.tensor_tensor(rprob[:], lexp[:], spread(linv[:]), ALU.mult))
                after(5)
                left = rprob
                for r in range(2):
                    n = 5 + 4 * r
                    step(dve.tensor_reduce(top[:, r, :], left[:], AX.X, ALU.max))
                    after(n + 1)
                    dve.tensor_tensor(tie[:, r], left[:], spread(top[:, r, :]), ALU.is_equal).then_inc(tie_ready, 1)
                    dve.wait_ge(tie_ready, pos(b, None, 2 * r + 1, 4))
                    dve.tensor_tensor(tie[:, r], tie[:, r], rank[:], ALU.mult).then_inc(tie_ready, 1)
                    dve.wait_ge(tie_ready, pos(b, None, 2 * r + 2, 4))
                    step(dve.tensor_reduce(first[:, r, :], tie[:, r], AX.X, ALU.max))
                    after(n + 2)
                    step(dve.tensor_tensor(chosen[:, r], tie[:, r], spread(first[:, r, :]), ALU.is_equal))
                    after(n + 3)
                    if r == 0:
                        step(dve.scalar_tensor_tensor(rest[:], chosen[:, 0], -4.0, rprob[:], ALU.mult, ALU.add))
                        left = rest
                        after(n + 4)
                step(dve.tensor_tensor(coef[:], chosen[:, 0], chosen[:, 1], ALU.add))
                after(13)
                step(dve.tensor_tensor(coef[:], coef[:], rprob[:], ALU.mult))
                assert done[0] == ROUTE

            with dve.Fori(0, B) as b:
                dve.tensor_copy(mod[:], mod_all[:, :, bass.ds(b, 1)].rearrange("p k b -> p (k b)")).then_inc(mod_picked, 1)
                dve.memset(attnT[:], 0.0).then_inc(outT_added, 1)
                dve.wait_ge(x_loaded, 16 * b + 16)
                normalise_rows(0, b, x_in)
                hT_lo(0, b)
                dve.wait_ge(outT_added, pos(b, None, 1, OUTS))
                walk(b, None, FIRST, -1)
                walk(b, None, STAGE, 0)
                with dve.Fori(0, LOOPED) as p:
                    walk(b, p, STAGE, 1)
                    walk(b, p, STAGE, 2)
                walk(b, None, STAGE, H - 1)
                walk(b, None, LAST, H)
                dve.wait_ge(outT_added, pos(b, None, OUTS, OUTS))
                dve.tensor_scalar(attnT[:], attnT[:], mod[:, GATE:GATE + 1], None, ALU.mult).then_inc(attn_gated, 1)
                for k in range(NBLK):
                    dve.wait_ge(attn_filled, pos(b, None, k + 1, NBLK))
                    tiles = slice(TPB * k, TPB * (k + 1))
                    dve.tensor_tensor(x_mid[:, tiles, :], ps[:, k, :].rearrange("p (t m) -> p t m", m=M), x_in[:, tiles, :],
                                      ALU.add).then_inc(x_mid_ready, 1)
                dve.wait_ge(x_mid_ready, pos(b, None, NBLK + 1, NBLK))
                normalise_rows(1, b, x_mid)
                hT_lo(1, b)
                route(b)
                for k in range(NBLK):
                    for g in range(PAIRS):
                        i = PAIRS * k + g
                        c = pos(b, None, i + 1, NBLK * PAIRS)
                        routed = g < EPAIRS
                        first_out = gated_buf(i) if routed else act_buf(i)
                        dve.wait_ge(up_filled, c)
                        dve.wait_ge(silu_ready, c)
                        if i >= 2:
                            dve.wait_ge(act_hi_ready, c - 2)
                        ins = dve.tensor_tensor(first_out, silu_buf(i), ps[:, 2 + i % 2, :], ALU.mult)
                        ins.then_inc(gated_ready, 1)
                        dve.wait_ge(gated_ready, c)
                        if routed:
                            dve.wait_ge(coefT_filled, pos(b, None, EPAIRS * k + g + 1, NBLK * EPAIRS))
                            dve.tensor_tensor(act_buf(i), gated_buf(i), ps[:, 5 + i % 2, :], ALU.mult).then_inc(act_ready, 1)
                        else:
                            dve.nop().then_inc(act_ready, 1)
                        dve.wait_ge(act_hi_ready, c)
                        dve.tensor_tensor(act_hl(1, g), act_buf(i), act_hl(0, g).bitcast(F32), ALU.subtract).then_inc(act_lo_ready, 1)
                    dve.wait_ge(y_turned, pos(b, None, k + 1, NBLK))
                    tiles = slice(TPB * k, TPB * (k + 1))
                    if k == 0:
                        dve.wait_ge(stored, b * 16 * NBLK + 16)
                    dve.tensor_tensor(out_sb[:, tiles, :], ps[:, 7, :].rearrange("p (t m) -> p t m", m=M), x_mid[:, tiles, :],
                                      ALU.add).then_inc(out_ready, 1)

        @block.tensor
        def _(pe):
            pe.wait_ge(c_ready, 1)
            for k in range(6):
                ins = pe.matmul(ps[:, 7, k * B:(k + 1) * B], st_mod[:, k, :], csilu[:], start=(k == 0), stop=(k == 5),
                                skip_group_check=True)
            ins.then_inc(mod_filled, 1)
            pe.wait_ge(vo_loaded, 32)
            for h in range(H):
                ins = pe.matmul(ps[:, h // 4, M * (h % 4):M * (h % 4 + 1)], st_vT[:, h, :], st_o[:, h, :], start=True, stop=True)
            ins.then_inc(wvo_filled, 1)
            pe.wait_ge(consts_ready, 2)
            pe.wait_ge(wffn_ready, 1)

            def product(dst, left, right, lcols, rcols, first=True, last=True, check=False):
                ins = None
                for k, (a, c) in enumerate(((0, 0), (0, 1), (1, 0))):
                    ins = pe.matmul(dst, lcols(left[a]), rcols(right[c]), start=first and k == 0, stop=last and k == 2,
                                    skip_group_check=check)
                return ins

            def turn_normed(i, b):
                for k in range(NBLK):
                    for t in range(TPB * k, TPB * (k + 1)):
                        pe.wait_ge(normed_ready, pos(b, None, TILES * i + t + 1, 2 * TILES))
                        ins = pe.transpose(ps[:, 2 + k, P * (t % TPB):P * (t % TPB + 1)], normed[:, t, :], ident[:])
                    ins.then_inc(normedT_filled, 1)

            def fill(b, p, unit):
                kind, n, t = unit[:3]
                bank = ps[:, bank_of(unit), :]
                if RI[unit] >= RING:
                    wait_ring(pe, ring_done, b, p, unit, back=RING)
                if kind == "P":
                    head = n if p is None else 2 * p + n
                    ins = product(bank[:, 0:QKV], hT_hl, wqkv, lambda a: a[:, P * t:P * (t + 1)], lambda a: a[:, head, :])
                elif kind == "R":
                    wait_tile(pe, rotated_ready, b, p, n, TPB * t + TPB - 1)
                    for j in range(TPB):
                        ins = pe.transpose(bank[:, P * j:P * (j + 1)], rotated[:, TPB * t + j, D * unit[3]:D * (unit[3] + 1)], ident[:])
                else:
                    j0 = TPB * unit[3]
                    wait_tile(pe, probs_ready, b, p, n, t)
                    for j in range(j0, min(j0 + TPB, t + 1)):
                        ins = pe.transpose(bank[:, P * (j - j0):P * (j - j0 + 1)], probs[:, t % 4, P * j:P * (j + 1)], ident[:])
                ins.then_inc(ring_filled, 1)

            def scores(b, p, n, t):
                at, pieces = score_cols(t)
                if (n, t) >= (0, 2):
                    m = (n, t - 2) if t >= 2 else (n - 1, t + TILES - 2)
                    wait_tile(pe, exp_ready, b, p, *m)
                if t % TPB == 0:
                    wait_ring(pe, ring_done, b, p, ("R", n, t // TPB, 1))
                pair = score_pair(t)
                for i, (dst, src, w) in enumerate(pieces):
                    product(pair[:, dst:dst + w], q_hl[n % 2], k_hl[n % 2], lambda a: a[:, P * t:P * (t + 1)],
                            lambda a: a[:, src:src + w], last=(i < len(pieces) - 1))
                end = at + (t + 1) * P
                pe.matmul(pair[:, end - P:end], identb[:], causalb[:], start=False, stop=True).then_inc(scores_filled, 1)

            def attend(b, p, n, k, j0, j1):
                if j0 == 0:
                    pe.wait_ge(outT_added, pos(b, p, NBLK * n + k + 1, OUTS, 2 * NBLK))
                    t = TPB * (k + 1) - 1
                    wait_ring(pe, ring_done, b, p, ("T", n, t, t // TPB))
                for j in range(j0, j1):
                    c0 = P * max(0, j - TPB * k)
                    ins = product(ps[:, OUT_BANK, c0:BLOCK], v_hl[n % 2], probsT[k], lambda a: a[:, j, :],
                                  lambda a: a[:, j, c0:BLOCK], first=(j == 0), last=(j == TPB * (k + 1) - 1))
                if j1 == TPB * (k + 1):
                    ins.then_inc(outT_filled, 1)

            def walk(b, p, text, n):
                for step in steps(text, n, H):
                    if step[0] == "S":
                        scores(b, p, *step[1:])
                    elif step[0] == "A":
                        attend(b, p, *step[1:])
                    elif step[0] in RING_STEPS:
                        fill(b, p, step)

            with pe.Fori(0, B) as b:
                turn_normed(0, b)
                pe.wait_ge(wqk_ready, 1)
                pe.wait_ge(wvo_ready, 1)
                pe.wait_ge(hT_lo_ready, pos(b, None, NBLK, 2 * NBLK))
                walk(b, None, FIRST, -1)
                walk(b, None, STAGE, 0)
                with pe.Fori(0, LOOPED) as p:
                    walk(b, p, STAGE, 1)
                    walk(b, p, STAGE, 2)
                walk(b, None, STAGE, H - 1)
                walk(b, None, LAST, H)
                pe.wait_ge(attn_gated, b + 1)
                for t in range(TILES):
                    ins = pe.transpose(ps[:, t // TPB, P * (t % TPB):P * (t % TPB + 1)], attnT[:, P * t:P * (t + 1)], ident[:])
                    if t % TPB == TPB - 1:
                        ins.then_inc(attn_filled, 1)
                turn_normed(1, b)
                for t in range(TILES):
                    if t % TPB == 0:
                        pe.wait_ge(hT_ready, pos(b, None, NBLK + t // TPB + 1, 2 * NBLK))
                    ins = pe.matmul(ps[:, 7, E * t:E * (t + 1)], hT[:, P * t:P * (t + 1)], router_sb[:], start=(t == 0),
                                    stop=(t == TILES - 1), skip_group_check=True)
                ins.then_inc(logits_filled, 1)

                def down(k, g):
                    i = PAIRS * k + g
                    if g == 0 and k > 0:
                        pe.wait_ge(yT_ready, pos(b, None, k, NBLK))
                    pe.wait_ge(act_lo_ready, pos(b, None, i + 1, NBLK * PAIRS))
                    ins = product(ps[:, 4, :], wdn, [act_hl(0, g), act_hl(1, g)], lambda a: a[:, g, :], lambda a: a,
                                  first=(g == 0), last=(g == PAIRS - 1))
                    if g == PAIRS - 1:
                        ins.then_inc(y_filled, 1)

                def turn_out(k):
                    pe.wait_ge(yT_ready, pos(b, None, k + 1, NBLK))
                    if k > 0:
                        pe.wait_ge(out_ready, pos(b, None, k, NBLK))
                    for t in range(TPB):
                        ins = pe.transpose(ps[:, 7, P * t:P * (t + 1)], yT[:, BLOCK * k + P * t:BLOCK * k + P * (t + 1)], ident[:])
                    ins.then_inc(y_turned, 1)

                for k in range(NBLK):
                    cols = slice(BLOCK * k, BLOCK * (k + 1))
                    pe.wait_ge(hT_lo_ready, pos(b, None, NBLK + k + 1, 2 * NBLK))
                    for g in range(PAIRS):
                        i = PAIRS * k + g
                        c = pos(b, None, i + 1, NBLK * PAIRS)
                        if i >= 2:
                            pe.wait_ge(silu_ready, c - 2)
                        product(ps[:, i % 2, :], wgu, hT_hl, lambda a: a[:, 2 * g, :], lambda a: a[:, cols]).then_inc(gate_filled, 1)
                        if i >= 2:
                            pe.wait_ge(gated_ready, c - 2)
                        product(ps[:, 2 + i % 2, :], wgu, hT_hl, lambda a: a[:, 2 * g + 1, :], lambda a: a[:, cols]).then_inc(up_filled, 1)
                        if g < EPAIRS:
                            pe.wait_ge(coef_spread, pos(b, None, EPAIRS * k + g + 1, NBLK * EPAIRS))
                            if i >= 2:
                                pe.wait_ge(act_ready, c - 2)
                            for t in range(TPB):
                                ins = pe.transpose(ps[:, 5 + i % 2, P * t:P * (t + 1)], coef_buf(EPAIRS * k + g)[:, t, :], ident[:])
                            ins.then_inc(coefT_filled, 1)
                        if g >= 1:
                            down(k, g - 1)
                    down(k, PAIRS - 1)
                    turn_out(k)


_OUT = (2, 1024, 128)


def kernel(**inputs):
    import concourse.bacc as _bacc
    from concourse.bass_utils import run_bass_kernel_spmd as _run

    a = {k: np.asarray(v) for k, v in inputs.items()}
    M, H, D = a["L0_attn_w_aq"].shape
    T = a["L0_attn_x"].shape[1]
    E = a["L0_ffn_router"].shape[1]
    half = D // 2
    freqs = np.power(np.float32(10000.0), -np.arange(half, dtype=np.float32) / np.float32(half)).astype(np.float32)
    radians = (np.arange(T, dtype=np.float32)[:, None] * freqs[None, :]).astype(np.float64)
    cos, sin = np.cos(radians).astype(np.float32), np.sin(radians).astype(np.float32)

    def by_tile(m):
        return m.reshape(T // P, P, m.shape[1]).transpose(1, 0, 2)

    gate, up = a["L0_ffn_experts_gate"], a["L0_ffn_experts_up"]
    pairs = [w for g in range(E // 2) for w in (np.concatenate([gate[2 * g], gate[2 * g + 1]], 1),
                                                np.concatenate([up[2 * g], up[2 * g + 1]], 1))]
    pairs += [a["L0_ffn_shared_gate"], a["L0_ffn_shared_up"]]
    down = a["L0_ffn_experts_down"]
    downs = [np.concatenate([down[2 * g], down[2 * g + 1]], 0) for g in range(E // 2)] + [a["L0_ffn_shared_down"]]
    arrays = {
        "x": a["L0_attn_x"],
        "w_qk": np.concatenate([a["L0_attn_w_aq"], a["L0_attn_w_ak"]], 2),
        "w_vT": a["L0_attn_w_av"].transpose(2, 1, 0),
        "w_o": a["L0_attn_w_ao"].transpose(1, 0, 2),
        "router": a["L0_ffn_router"],
        "w_gate_up": np.stack(pairs, 1),
        "w_down": np.stack(downs, 1),
        "cT": a["L0_c"].T,
        "w_mod": a["L0_wmod"].reshape(M, 6, M),
        "cos_t": by_tile(cos),
        "sin_t": by_tile(np.concatenate([-sin, sin], 1)),
        "causal": np.where(np.arange(P)[None, :] > np.arange(P)[:, None], np.float32(-1e30), np.float32(0)),
        "ident_in": np.eye(P, dtype=np.float32),
    }
    nc = _bacc.Bacc("TRN2", target_bir_lowering=False, num_devices=1)
    fed, aps = {}, []
    for name, arr in arrays.items():
        arr = np.ascontiguousarray(arr)
        fed[f"in_{name}"] = arr
        aps.append(nc.dram_tensor(f"in_{name}", arr.shape, mybir.dt.from_np(arr.dtype), kind="ExternalInput").ap())
    aps.append(nc.dram_tensor("out_dram", _OUT, F32, kind="ExternalOutput").ap())
    build(nc, *aps)
    r = _run(nc, [fed], core_ids=[0])
    return r.results[0]["out_dram"]
```

```python
from contextlib import ExitStack

import numpy as np

import concourse.bass as bass
from concourse import mybir

F32 = mybir.dt.float32
F32R = mybir.dt.float32r
BF16 = mybir.dt.bfloat16
ALU = mybir.AluOpType
ACT = mybir.ActivationFunctionType
AX = mybir.AxisListType

P = 128
RING = 3
B, H = 2, 8
NBLK = 2
PAIRS = 5
GROUPS = B * NBLK * PAIRS
EPS = 1e-5
ROUTE = 14
BLOCK = 512
TPB = BLOCK // P
SHIFT, SCALE, GATE = 0, 1, 2


HEAD_STEPS = "SXINTAOPR"
STAGE = """
T' 5 0; A' 0 0 1; N' 7; A' 0 1 2; I' 7; S 0; T' 5 1; X 0
T' 6 0; A' 0 2 4; S 1; I 0; T' 6 1; N 0; T' 7 0
S 2; N 1; O' 0; I 1; X 1; T' 7 1; X 2
S 3; R 1 0; R 1 1; A' 1 0 2; P+ 0; T 0 0; I 2; N 2; A' 1 2 3; P+ 1; N 3; X 3
S 4; I 3; T 1 0; X 4; P+ 2; A' 1 3 4
S 5; A' 1 4 5; P+ 3; I 4; T 2 0; N 4
S 6; A' 1 5 6; X 5; P+ 4; N 5; I 5; P+ 5; A' 1 6 7; T 3 0; X 6; N 6; A' 1 7 8
S 7; P+ 6; I 6; R+ 0 0; T 4 0; O' 1; X 7; T 4 1; P+ 7; R+ 0 1
"""
START = """
M 0 0; M 0 1; Z 0; W 0; Y 0 0; L 0 0; Y 0 1; L 0 1
P+ 0; P+ 1; P+ 2; P+ 3; W 1; P+ 4; P+ 5; R+ 0 0; R+ 0 1; P+ 6; P+ 7; K
"""
NEXT = {
    0: {1: "M 1 0", 2: "M 1 1; Z 1", 5: "Y 1 0", 6: "Y 1 1"},
    H - 1: {0: "L 1 0", 1: "L 1 1"},
    B * H - 1: {0: "G 0 0; G 0 1", 1: "F 0 0; M 2 0", 2: "F 0 1; M 2 1; Z 2", 3: "Y 2 0; Y 2 1", 4: "L 2 0",
                5: "L 2 1", 6: "E 0", 7: "J 0 0; J 0 1"},
}
LAST = """
I' 7; T' 5 0; N' 7; A' 0 0 1; T' 5 1; A' 0 1 2; J 0 2; T' 6 0; T' 6 1; A' 0 2 4; J 0 3; T' 7 0; T' 7 1; O' 0; G 1 0; J 0 4
A' 1 0 8; O' 1; G 1 1
"""
BETWEEN = {0: "F 1 0; M 3 0", 1: "F 1 1; M 3 1; Z 3", 2: "Y 3 0; L 3 0", 3: "Y 3 1; L 3 1", 4: "E 1; J 1 0",
           5: "J 1 1", 6: "J 1 2", 7: "J 1 3", 8: "J 1 4"}
RING_STEPS = "TPRLFECB"
SPLIT_STEPS = "TPRL"


def stage_text(n):
    slots = STAGE.strip().split("\n")
    return "; ".join((NEXT[n][i] + "; " if i in NEXT.get(n, {}) else "") + slot for i, slot in enumerate(slots))


def expert_text():
    out = []
    for i in range(GROUPS + 3):
        if i < GROUPS:
            out.append(f"U {i}")
            if i % PAIRS:
                out.append(f"C {i}")
        if 0 <= i - 1 < GROUPS:
            out.append(f"H {i - 1}")
        if 0 <= i - 2 < GROUPS:
            out.append(f"D {i - 2}")
            if (i - 2) % PAIRS == PAIRS - 1:
                out.append(f"Q {(i - 2) // PAIRS}")
        if i >= 3 and (i - 3) % PAIRS == PAIRS - 1:
            out.append(f"B {(i - 3) // PAIRS}")
        if i in BETWEEN:
            out.append(BETWEEN[i])
    return "; ".join(out)


def steps(text, n):
    for step in text.replace("\n", ";").split(";"):
        if step.strip():
            name, *rest = step.split()
            rest = tuple(map(int, rest))
            if name[0] not in HEAD_STEPS:
                yield (name[0],) + rest
            else:
                head = n + {"'": -1, "+": 1}.get(name[1:], 0)
                if 0 <= head < B * H:
                    yield (name[0], head) + rest


def ring_plan(kinds):
    texts = [(START, -1)] + [(stage_text(n), n) for n in range(B * H)] + [(LAST, B * H), (expert_text(), None)]
    every = [s for text, n in texts for s in steps(text, n)]
    return {s: i for i, s in enumerate(s for s in every if s[0] in kinds)}


def build(nc, x, w_qk, w_vT, w_o, router, w_gate_up, w_down, cT, w_mod, cos_t, sin_t, causal, ident_in, out):
    _, T, M = x.shape
    D = w_qk.shape[2] // 2
    E = router.shape[1]
    TILES = T // P
    HALF = D // 2
    QKV = 3 * D
    EPAIRS = E // 2
    SM = 1.0 / D
    assert (M, D, TILES, NBLK * BLOCK) == (P, P, 8, T)
    assert (B, H, PAIRS) == (x.shape[0], w_qk.shape[1], w_down.shape[1])
    LOOPED = (H - 2) // 2
    RI = ring_plan(RING_STEPS)
    SPLIT = ring_plan(SPLIT_STEPS)
    PER = RI[("T", 3, 0, 0)] - RI[("T", 1, 0, 0)]
    assert PER % RING == 0

    with ExitStack() as ctx:
        def sb(name, shape, dt=F32):
            return ctx.enter_context(nc.sbuf_tensor(name, shape, dt))

        def sem(name):
            return ctx.enter_context(nc.semaphore(name))

        ps = ctx.enter_context(nc.psum_tensor("ps", [P, 8, BLOCK], F32))
        OUT_BANK, RING0 = 4, 5

        wqkv = [sb(f"wqkv_{s}", [P, H, QKV], F32R) for s in ("hi", "lo")]
        wgu = [sb(f"wgu_{s}", [P, 2 * PAIRS, P], F32R) for s in ("hi", "lo")]
        wdn = [sb(f"wdn_{s}", [P, PAIRS, P], F32R) for s in ("hi", "lo")]
        router_sb = sb("router_sb", [P, E])
        cos_sb = sb("cos_sb", [P, TILES, HALF])
        sin_sb = sb("sin_sb", [P, TILES, D])
        ident = sb("ident", [P, P])
        identb = sb("identb", [P, P], BF16)
        causalb = sb("causalb", [P, P], BF16)
        c_sb = sb("c_sb", [P, B])
        csilu = sb("csilu", [P, B])
        mod_all = sb("mod_all", [P, 6, B])
        mod_sign = sb("mod_sign", [P, 2, B])
        mod_size = sb("mod_size", [P, 2, B])
        rows = sb("rows", [P, B, TILES, M])
        stats = sb("stats", [P, TILES, 6])
        mean_sum = sb("mean_sum", [P, TILES])
        mean_gap = sb("mean_gap", [P, TILES])
        mean = sb("mean", [P, TILES])
        gap2 = sb("gap2", [P, TILES])
        squares = sb("squares", [P, TILES])
        squares2 = sb("squares2", [P, TILES])
        vareps = sb("vareps", [P, TILES])
        minus_half = sb("minus_half", [P, TILES])
        rstd = sb("rstd", [P, TILES])
        normed = sb("normed", [P, TILES, M])
        hT = sb("hT", [P, T])
        hT_hl = [sb(f"hT_{s}", [P, T], F32R) for s in ("hi", "lo")]
        q_hl = [[sb(f"q_{s}{k}", [P, T], F32R) for s in ("hi", "lo")] for k in range(2)]
        k_hl = [[sb(f"k_{s}{k}", [P, T], F32R) for s in ("hi", "lo")] for k in range(2)]
        v_hl = [[sb(f"v_{s}{k}", [P, TILES, M], F32R) for s in ("hi", "lo")] for k in range(2)]
        qk_raw = sb("qk_raw", [P, 2, 2 * D])
        cos_part = sb("cos_part", [P, 2, 2 * D])
        sin_part = sb("sin_part", [P, 2, 2 * D])
        rotated = sb("rotated", [P, TILES, 2 * D])
        probs = sb("probs", [P, 4, T])
        probsT = [[sb(f"probsT{k}_{s}", [P, TPB * (k + 1), BLOCK], F32R) for s in ("hi", "lo")] for k in range(NBLK)]
        neg_max = sb("neg_max", [P, TILES])
        row_sum = sb("row_sum", [P, TILES])
        inv_sum = sb("inv_sum", [P, TILES])
        attnT = sb("attnT", [P, B, T])
        lmax = sb("lmax", [P, TILES])
        lsub = sb("lsub", [P, TILES, E])
        lexp = sb("lexp", [P, TILES, E])
        lsum = sb("lsum", [P, TILES])
        linv = sb("linv", [P, TILES])
        rprob = sb("rprob", [P, TILES, E])
        rank = sb("rank", [P, TILES, E])
        top = sb("top", [P, 2, TILES])
        tie = sb("tie", [P, 2, TILES, E])
        first = sb("first", [P, 2, TILES])
        chosen = sb("chosen", [P, 2, TILES, E])
        rest = sb("rest", [P, TILES, E])
        coef = sb("coef", [P, B, TILES, E])

        st_qk = probs[:, 0:2, :].rearrange("p a (h d) -> p (a h) d", d=2 * D)
        st_vT = probs[:, 2, :].rearrange("p (h d) -> p h d", d=D)
        st_o = probs[:, 3, :].rearrange("p (h d) -> p h d", d=M)
        st_mod = hT[:, 0:6 * M].rearrange("p (k d) -> p k d", d=M)
        st_ffn = attnT[:].rearrange("p b t -> p (b t)")
        st_gu = st_ffn[:, 0:2 * PAIRS * P].rearrange("p (g d) -> p g d", d=P)
        st_dn = st_ffn[:, 2 * PAIRS * P:3 * PAIRS * P].rearrange("p (g d) -> p g d", d=P)
        causal_f = st_ffn[:, 3 * PAIRS * P:3 * PAIRS * P + P]
        def silu_buf(i):
            return probs[:, 0, (i % 2) * BLOCK:(i % 2 + 1) * BLOCK]

        def gated_buf(i):
            return probs[:, 1, (i % 2) * BLOCK:(i % 2 + 1) * BLOCK]

        def act_buf(i):
            return probs[:, 2, (i % 2) * BLOCK:(i % 2 + 1) * BLOCK]

        def act_hl(i):
            return [probsT[1][s][:, i % TILES, :] for s in (0, 1)]

        def coef_buf(i):
            return rotated[:, 2 * (i % 4):2 * (i % 4) + 2, :].rearrange("p a (t d) -> p (a t) d", d=P)

        def yT(j):
            return probs[:, 3, (j % 2) * BLOCK:(j % 2 + 1) * BLOCK]

        norm_hl = [hT_hl, hT_hl, hT_hl, q_hl[0]]

        x_loaded = sem("x_loaded")
        x_last_loaded = sem("x_last_loaded")
        qk_loaded = sem("qk_loaded")
        vo_loaded = sem("vo_loaded")
        mod_loaded = sem("mod_loaded")
        ident_loaded = sem("ident_loaded")
        tables_loaded = sem("tables_loaded")
        ffn_loaded = sem("ffn_loaded")
        pool_consts_ready = sem("pool_consts_ready")
        consts_ready = sem("consts_ready")
        c_ready = sem("c_ready")
        mod_filled = sem("mod_filled")
        mod_steps = sem("mod_steps")
        wvo_filled = sem("wvo_filled")
        w_hi_ready = sem("w_hi_ready")
        w_ready = sem("w_ready")
        wffn_hi_ready = sem("wffn_hi_ready")
        wffn_ready = sem("wffn_ready")
        stats_ready = sem("stats_ready")
        halves_ready = sem("halves_ready")
        var_steps = sem("var_steps")
        pool_waits = sem("pool_waits")
        vareps_ready = sem("vareps_ready")
        rstd_ready = sem("rstd_ready")
        normed_ready = sem("normed_ready")
        hT_ready = sem("hT_ready")
        ring_filled = sem("ring_filled")
        ring_hi_ready = sem("ring_hi_ready")
        ring_done = sem("ring_done")
        sin_ready = sem("sin_ready")
        rotated_ready = sem("rotated_ready")
        scores_filled = sem("scores_filled")
        max_ready = sem("max_ready")
        exp_ready = sem("exp_ready")
        inv_ready = sem("inv_ready")
        probs_ready = sem("probs_ready")
        outT_filled = sem("outT_filled")
        outT_added = sem("outT_added")
        attn_gated = sem("attn_gated")
        x_mid_ready = sem("x_mid_ready")
        route_steps = sem("route_steps")
        route_exp = sem("route_exp")
        tie_ready = sem("tie_ready")
        coef_spread = sem("coef_spread")
        gate_filled = sem("gate_filled")
        up_filled = sem("up_filled")
        silu_ready = sem("silu_ready")
        gated_ready = sem("gated_ready")
        act_ready = sem("act_ready")
        act_hi_ready = sem("act_hi_ready")
        act_lo_ready = sem("act_lo_ready")
        y_filled = sem("y_filled")
        yT_ready = sem("yT_ready")
        out_ready = sem("out_ready")
        stored = sem("stored")

        def pos(p, count, per_pair):
            return count if p is None else count + p * per_pair

        def wait_tile(eng, s, p, n, t):
            eng.wait_ge(s, pos(p, TILES * n + t + 1, 2 * TILES))

        def wait_ring(eng, s, p, unit, back=0):
            order = SPLIT if s is ring_hi_ready else RI
            eng.wait_ge(s, pos(p, order[unit] + 1 - back, PER))

        def bank_of(unit):
            return ps[:, RING0 + RI[unit] % RING, :]

        def tiles_of(k):
            return slice(TPB * k, TPB * (k + 1))

        def cols_of(k):
            return slice(BLOCK * k, BLOCK * (k + 1))

        def group(i):
            j, place = divmod(i, PAIRS)
            return j // NBLK, j % NBLK, (place - 1) % PAIRS

        def coef_index(i):
            return EPAIRS * (i // PAIRS) + i % PAIRS - 1

        def all_stages(eng, walk):
            walk(None, START, -1)
            for b in range(B):
                n = b * H
                walk(None, stage_text(n), n)
                with eng.Fori(0, LOOPED) as p:
                    walk(p, stage_text(n + 1), n + 1)
                    walk(p, stage_text(n + 2), n + 2)
                walk(None, stage_text(n + H - 1), n + H - 1)
            walk(None, LAST, B * H)
            walk(None, expert_text(), None)

        def score_cols(t):
            w = (t + 1) * P
            if w == BLOCK + P:
                return P, [(P, 0, 3 * P), (BLOCK, 3 * P, 2 * P)]
            return 0, [(c, c, min(BLOCK, w - c)) for c in range(0, w, BLOCK)]

        def score_pair(t):
            return ps[:, 2 * (t % 2):2 * (t % 2) + 2, :].rearrange("p a c -> p (a c)")

        def view(ap, dims, offset=0):
            return bass.AP(ap.tensor, ap.offset + offset, [ap.ap[0]] + dims)

        block = ctx.enter_context(nc.Block())

        @block.sync
        def _(sp):
            sp.dma_start(c_sb[:], cT).then_inc(mod_loaded, 16)
            sp.dma_start(st_mod, w_mod).then_inc(mod_loaded, 16)
            sp.dma_start(rows[:, 0], x[0].rearrange("(t p) m -> p t m", p=P)).then_inc(x_loaded, 16)
            sp.dma_start(ident[:], ident_in).then_inc(ident_loaded, 16)
            sp.dma_start(st_qk, w_qk).then_inc(qk_loaded, 16)
            sp.dma_start(cos_sb[:], cos_t).then_inc(tables_loaded, 16)
            sp.dma_start(sin_sb[:], sin_t).then_inc(tables_loaded, 16)
            sp.dma_start(causal_f, causal).then_inc(tables_loaded, 16)
            sp.dma_start(rows[:, 1], x[1].rearrange("(t p) m -> p t m", p=P)).then_inc(x_last_loaded, 16)
            for j in range(B * NBLK):
                b, k = divmod(j, NBLK)
                sp.wait_ge(out_ready, j + 1)
                sp.dma_start(out[b].rearrange("(k t p) m -> k p t m", p=P, t=TPB)[k],
                             rows[:, b, tiles_of(k), :]).then_inc(stored, 16)
            sp.wait_ge(stored, 16 * B * NBLK)

        @block.gpsimd
        def _(pool):
            pool.dma_start(st_vT, w_vT).then_inc(vo_loaded, 16)
            pool.dma_start(st_o, w_o).then_inc(vo_loaded, 16)
            pool.memset(minus_half[:], -0.5)
            pool.dma_start(st_gu, w_gate_up).then_inc(ffn_loaded, 16)
            pool.dma_start(st_dn, w_down).then_inc(ffn_loaded, 16)
            pool.dma_start(router_sb[:], router).then_inc(ffn_loaded, 16)
            for e in range(E):
                ins = pool.memset(rank[:, :, e], float(E - e))
            ins.then_inc(pool_consts_ready, 1)

            def split_experts():
                pool.wait_ge(ffn_loaded, 48)
                pool.tensor_scalar(wgu[0][:], st_gu, 1.0, 1.0, ALU.mult, ALU.mult)
                pool.tensor_scalar(wdn[0][:], st_dn, 1.0, 1.0, ALU.mult, ALU.mult).then_inc(wffn_hi_ready, 1)
                pool.wait_ge(wffn_hi_ready, 1)
                pool.tensor_tensor(wgu[1][:], st_gu, wgu[0][:].bitcast(F32), ALU.subtract)
                pool.tensor_tensor(wdn[1][:], st_dn, wdn[0][:].bitcast(F32), ALU.subtract).then_inc(wffn_ready, 1)
                pool.wait_ge(wffn_ready, 1)
                pool.wait_ge(consts_ready, 1)
                pool.memset(attnT[:], 0.0).then_inc(outT_added, 1)

            def rstd_step(i):
                if i == 0:
                    pool.wait_ge(pool_consts_ready, 1)
                pool.wait_ge(vareps_ready, i + 1)
                pool.tensor_tensor(rstd[:], vareps[:], minus_half[:], ALU.pow).then_inc(rstd_ready, 1)

            def rotate(p, n, t):
                unit = ("P", n, t)
                if (n, t) == (0, 0):
                    pool.wait_ge(tables_loaded, 48)
                raw = qk_raw[:, t % 2, :]
                swapped = view(raw, [[D, 2], [-HALF, 2], [1, HALF]], HALF)
                wait_ring(pool, ring_hi_ready, p, unit)
                pool.tensor_tensor(view(sin_part[:, t % 2, :], [[D, 2], [HALF, 2], [1, HALF]]), swapped,
                                   view(sin_sb[:, t, :], [[0, 2], [HALF, 2], [1, HALF]]), ALU.mult).then_inc(sin_ready, 1)
                wait_tile(pool, sin_ready, p, n, t)
                wait_ring(pool, ring_done, p, unit)
                pool.tensor_tensor(rotated[:, t, :], cos_part[:, t % 2, :], sin_part[:, t % 2, :],
                                   ALU.add).then_inc(rotated_ready, 1)

            def normalise(p, n, t):
                w = (t + 1) * P
                wait_tile(pool, inv_ready, p, n, t)
                pool.sem_inc(pool_waits, 1)
                pool.tensor_scalar(probs[:, t % 4, 0:w], probs[:, t % 4, 0:w], inv_sum[:, t:t + 1], 1.0,
                                   ALU.mult, ALU.mult).then_inc(probs_ready, 1)

            def spread_coef(i):
                b, k, g = group(i)
                c = coef_index(i)
                pool.wait_ge(route_steps, ROUTE * (b + 1))
                if c >= EPAIRS:
                    wait_ring(pool, ring_filled, None, ("C", i - PAIRS))
                pool.sem_inc(pool_waits, 1)
                pool.tensor_scalar(coef_buf(c).rearrange("p t (e d) -> p t e d", e=2),
                                   view(coef[:, b, TPB * k, 2 * g:2 * g + 2], [[E, TPB], [1, 2], [0, P // 2]]),
                                   1.0, 1.0, ALU.mult, ALU.mult).then_inc(coef_spread, 1)

            def walk(p, text, n):
                for name, *of in steps(text, n):
                    if name == "N":
                        normalise(p, *of)
                    elif name == "P":
                        rotate(p, *of)
                    elif name == "K":
                        split_experts()
                    elif name == "Z":
                        rstd_step(*of)
                    elif name == "C":
                        spread_coef(*of)

            all_stages(pool, walk)

        @block.scalar
        def _(act):
            act.wait_ge(mod_loaded, 32)
            act.activation(csilu[:], c_sb[:], ACT.Silu).then_inc(c_ready, 1)

            def split_weights(s):
                heads = (slice(0, 1), slice(1, H))[s]
                if s == 0:
                    act.wait_ge(qk_loaded, 16)
                    act.wait_ge(wvo_filled, 1)
                wvo = ps[:, 0:2, :].rearrange("p a (h m) -> p (a h) m", m=M)
                act.copy(wqkv[0][:, heads, 0:2 * D], st_qk[:, heads, :])
                act.copy(wqkv[0][:, heads, 2 * D:QKV], wvo[:, heads, :]).then_inc(w_hi_ready, 1)

            def constants():
                act.wait_ge(ident_loaded, 16)
                act.wait_ge(tables_loaded, 48)
                act.copy(identb[:], ident[:])
                act.copy(causalb[:], causal_f).then_inc(consts_ready, 1)

            def modulate(i, k):
                which, b = divmod(i, B)
                unit = ("L", i, k)
                wait_ring(act, ring_filled, None, unit)
                if (i, k) == (0, 0):
                    act.wait_ge(mod_steps, 6)
                act.activation(hT[:, cols_of(k)], bank_of(unit), ACT.Identity,
                               bias=mod_all[:, 3 * which + SHIFT, b:b + 1],
                               scale=mod_all[:, 3 * which + SCALE, b:b + 1]).then_inc(hT_ready, 1)
                act.wait_ge(hT_ready, NBLK * i + k + 1)
                act.copy(norm_hl[i][0][:, cols_of(k)], hT[:, cols_of(k)]).then_inc(ring_hi_ready, 1)

            def exponent(p, n, t):
                at, _ = score_cols(t)
                w = (t + 1) * P
                wait_tile(act, max_ready, p, n, t)
                act.activation(probs[:, t % 4, 0:w], score_pair(t)[:, at:at + w], ACT.Exp, bias=neg_max[:, t:t + 1],
                               accum_out=row_sum[:, t:t + 1]).then_inc(exp_ready, 1)

            def take_hi(p, unit):
                kind, n, t = unit[:3]
                bank = bank_of(unit)
                if kind == "P":
                    if (n, t) >= (0, 2):
                        m = (n, t - 2) if t >= 2 else (n - 1, t + TILES - 2)
                        wait_tile(act, sin_ready, p, *m)
                    wait_ring(act, ring_filled, p, unit)
                    act.copy(qk_raw[:, t % 2, :], bank[:, 0:2 * D])
                    act.copy(v_hl[n % 2][0][:, t, :], bank[:, 2 * D:QKV]).then_inc(ring_hi_ready, 1)
                elif kind == "R":
                    wait_ring(act, ring_filled, p, unit)
                    act.activation((q_hl, k_hl)[unit[3]][n % 2][0][:, cols_of(t)], bank, ACT.Copy,
                                   scale=(SM, 1.0)[unit[3]]).then_inc(ring_hi_ready, 1)
                else:
                    j0 = TPB * unit[3]
                    k = min(TPB, t + 1 - j0)
                    wait_ring(act, ring_filled, p, unit)
                    act.copy(probsT[t // TPB][0][:, j0:j0 + k, P * (t % TPB):P * (t % TPB + 1)],
                             bank[:, 0:k * P].rearrange("p (j i) -> p j i", i=P)).then_inc(ring_hi_ready, 1)

            def route_exponent(b):
                act.wait_ge(route_steps, ROUTE * b + 2)
                act.activation(lexp[:], lsub[:], ACT.Exp).then_inc(route_exp, 1)

            def silu(i):
                act.wait_ge(gate_filled, i + 1)
                if i >= 2:
                    act.wait_ge(gated_ready, i - 1)
                act.activation(silu_buf(i), ps[:, i % 2, :], ACT.Silu).then_inc(silu_ready, 1)

            def activation_hi(i):
                act.wait_ge(act_ready, i + 1)
                act.copy(act_hl(i)[0], act_buf(i)).then_inc(act_hi_ready, 1)

            def gate_output(j):
                act.wait_ge(y_filled, j + 1)
                act.activation(yT(j), ps[:, OUT_BANK, :], ACT.Copy,
                               scale=mod_all[:, 3 + GATE, j // NBLK:j // NBLK + 1]).then_inc(yT_ready, 1)

            def walk(p, text, n):
                for step in steps(text, n):
                    name, *of = step
                    if name == "X":
                        exponent(p, *of)
                    elif name in "TPR":
                        take_hi(p, step)
                    elif name == "W":
                        split_weights(*of)
                    elif name == "K":
                        constants()
                    elif name == "L":
                        modulate(*of)
                    elif name == "J" and of[1] == 0:
                        route_exponent(of[0])
                    elif name == "U":
                        silu(*of)
                    elif name == "H":
                        activation_hi(*of)
                    elif name == "Q":
                        gate_output(*of)

            all_stages(act, walk)

        @block.vector
        def _(dve):
            def modulations():
                dve.wait_ge(mod_filled, 1)
                dve.tensor_copy(mod_all[:], ps[:, RING0, 0:6 * B].rearrange("p (k b) -> p k b", b=B)).then_inc(mod_steps, 1)
                dve.wait_ge(mod_steps, 1)
                scales = view(mod_all[:], [[3 * B, 2], [1, B]], SCALE * B)
                gates = view(mod_all[:], [[3 * B, 2], [1, B]], GATE * B)
                dve.tensor_scalar(scales, scales, 1.0, None, ALU.add).then_inc(mod_steps, 1)
                dve.tensor_scalar(mod_sign[:], gates, 0.0, 2.0, ALU.is_ge, ALU.mult).then_inc(mod_steps, 1)
                dve.scalar_tensor_tensor(mod_size[:], gates, -1.0, gates, ALU.mult, ALU.max).then_inc(mod_steps, 1)
                dve.wait_ge(mod_steps, 4)
                dve.tensor_scalar(mod_sign[:], mod_sign[:], -1.0, None, ALU.add).then_inc(mod_steps, 1)
                dve.wait_ge(mod_steps, 5)
                dve.scalar_tensor_tensor(gates, mod_size[:], 0.25, mod_sign[:], ALU.max, ALU.mult).then_inc(mod_steps, 1)

            def split_weights(s):
                heads = (slice(0, 1), slice(1, H))[s]
                wvo = ps[:, 0:2, :].rearrange("p a (h m) -> p (a h) m", m=M)
                dve.wait_ge(w_hi_ready, s + 1)
                dve.tensor_tensor(wqkv[1][:, heads, 0:2 * D], st_qk[:, heads, :],
                                  wqkv[0][:, heads, 0:2 * D].bitcast(F32), ALU.subtract)
                dve.tensor_tensor(wqkv[1][:, heads, 2 * D:QKV], wvo[:, heads, :],
                                  wqkv[0][:, heads, 2 * D:QKV].bitcast(F32), ALU.subtract).then_inc(w_ready, 1)

            def statistics(i, k):
                which, b = divmod(i, B)
                if k == 0 and which == 0:
                    dve.wait_ge((x_loaded, x_last_loaded)[b], 16)
                if which == 1:
                    dve.wait_ge(x_mid_ready, NBLK * b + k + 1)
                for t in range(TPB * k, TPB * (k + 1)):
                    ins = dve.bn_stats(stats[:, t, :], rows[:, b, t, :])
                ins.then_inc(stats_ready, 1)

            def mean_and_variance(i):
                dve.wait_ge(stats_ready, NBLK * (i + 1))
                dve.tensor_tensor(mean_sum[:], stats[:, :, 1], stats[:, :, 4], ALU.add)
                dve.tensor_tensor(mean_gap[:], stats[:, :, 1], stats[:, :, 4], ALU.subtract)
                dve.tensor_tensor(squares[:], stats[:, :, 2], stats[:, :, 5], ALU.add).then_inc(halves_ready, 1)
                dve.wait_ge(halves_ready, i + 1)
                dve.tensor_scalar(mean[:], mean_sum[:], 0.5, None, ALU.mult)
                dve.scalar_tensor_tensor(gap2[:], mean_gap[:], 0.25, mean_gap[:], ALU.mult, ALU.mult)
                dve.tensor_scalar(squares2[:], squares[:], 1.0 / M, EPS, ALU.mult, ALU.add).then_inc(var_steps, 1)
                dve.wait_ge(var_steps, i + 1)
                dve.tensor_tensor(vareps[:], gap2[:], squares2[:], ALU.add).then_inc(vareps_ready, 1)

            def normalise_rows(i, k):
                b = i % B
                dve.wait_ge(rstd_ready, i + 1)
                for t in range(TPB * k, TPB * (k + 1)):
                    ins = dve.tensor_scalar(normed[:, t, :], rows[:, b, t, :], mean[:, t:t + 1], rstd[:, t:t + 1],
                                            ALU.subtract, ALU.mult)
                ins.then_inc(normed_ready, 1)

            def row_max(p, n, t):
                at, _ = score_cols(t)
                wait_tile(dve, scores_filled, p, n, t)
                dve.tensor_reduce(neg_max[:, t:t + 1], score_pair(t)[:, at:at + (t + 1) * P], AX.X, ALU.max,
                                  negate=True).then_inc(max_ready, 1)

            def invert(p, n, t):
                wait_tile(dve, exp_ready, p, n, t)
                dve.reciprocal(inv_sum[:, t:t + 1], row_sum[:, t:t + 1]).then_inc(inv_ready, 1)

            def take_lo(p, unit):
                kind, n, t = unit[:3]
                bank = bank_of(unit)
                if kind == "P":
                    if (n, t) == (0, 0):
                        dve.wait_ge(tables_loaded, 48)
                    if (n, t) >= (0, 2):
                        m = (n, t - 2) if t >= 2 else (n - 1, t + TILES - 2)
                        wait_tile(dve, rotated_ready, p, *m)
                    wait_ring(dve, ring_hi_ready, p, unit)
                    dve.tensor_tensor(view(cos_part[:, t % 2, :], [[HALF, 4], [1, HALF]]), view(bank, [[HALF, 4], [1, HALF]]),
                                      view(cos_sb[:, t, :], [[0, 4], [1, HALF]]), ALU.mult)
                    dve.tensor_tensor(v_hl[n % 2][1][:, t, :], bank[:, 2 * D:QKV], v_hl[n % 2][0][:, t, :].bitcast(F32),
                                      ALU.subtract).then_inc(ring_done, 1)
                elif kind == "R":
                    hi, lo = ((q_hl, k_hl)[unit[3]][n % 2][s][:, cols_of(t)] for s in (0, 1))
                    wait_ring(dve, ring_hi_ready, p, unit)
                    dve.scalar_tensor_tensor(lo, bank, (SM, 1.0)[unit[3]], hi.bitcast(F32), ALU.mult,
                                             ALU.subtract).then_inc(ring_done, 1)
                elif kind == "L":
                    hi, lo = (part[:, cols_of(t)] for part in norm_hl[n])
                    wait_ring(dve, ring_hi_ready, None, unit)
                    dve.tensor_tensor(lo, hT[:, cols_of(t)], hi.bitcast(F32), ALU.subtract).then_inc(ring_done, 1)
                else:
                    j0 = TPB * unit[3]
                    k = min(TPB, t + 1 - j0)
                    hi, lo = (probsT[t // TPB][s][:, j0:j0 + k, P * (t % TPB):P * (t % TPB + 1)] for s in (0, 1))
                    wait_ring(dve, ring_hi_ready, p, unit)
                    dve.tensor_tensor(lo, bank[:, 0:k * P].rearrange("p (j i) -> p j i", i=P), hi.bitcast(F32),
                                      ALU.subtract).then_inc(ring_done, 1)

            def add_out(p, n, k):
                part = attnT[:, n // H, cols_of(k)]
                dve.wait_ge(outT_filled, pos(p, NBLK * n + k + 1, 2 * NBLK))
                dve.tensor_tensor(part, part, ps[:, OUT_BANK, :], ALU.add).then_inc(outT_added, 1)

            def gate_attention(b, k):
                part = attnT[:, b, cols_of(k)]
                dve.wait_ge(outT_added, NBLK * (H * b + H - 1) + k + 2)
                dve.tensor_scalar(part, part, mod_all[:, GATE, b:b + 1], None, ALU.mult).then_inc(attn_gated, 1)

            def add_rows(b, k, unit):
                part = rows[:, b, tiles_of(k), :]
                ready, count = (x_mid_ready, NBLK * b + k + 1) if unit[0] == "F" else (out_ready, unit[1] + 1)
                wait_ring(dve, ring_filled, None, unit)
                dve.tensor_tensor(part, bank_of(unit).rearrange("p (t m) -> p t m", m=M), part, ALU.add).then_inc(ready, 1)
                dve.wait_ge(ready, count)
                dve.sem_inc(ring_done, 1)

            def spread(a):
                return view(a, [[1, TILES], [0, E]])

            def router_logits(b):
                unit = ("E", b)
                logits = bank_of(unit)[:, 0:TILES * E].rearrange("p (t e) -> p t e", e=E)
                wait_ring(dve, ring_filled, None, unit)
                dve.tensor_reduce(lmax[:], logits, AX.X, ALU.max).then_inc(route_steps, 1)
                dve.wait_ge(route_steps, ROUTE * b + 1)
                dve.tensor_tensor(lsub[:], logits, spread(lmax[:]), ALU.subtract).then_inc(route_steps, 1)
                dve.wait_ge(route_steps, ROUTE * b + 2)
                dve.sem_inc(ring_done, 1)

            def route(b, part):
                def after(n):
                    dve.wait_ge(route_steps, ROUTE * b + n)

                if part == 1:
                    dve.wait_ge(route_exp, b + 1)
                    dve.tensor_reduce(lsum[:], lexp[:], AX.X, ALU.add).then_inc(route_steps, 1)
                    after(3)
                    dve.reciprocal(linv[:], lsum[:]).then_inc(route_steps, 1)
                    after(4)
                    dve.tensor_tensor(rprob[:], lexp[:], spread(linv[:]), ALU.mult).then_inc(route_steps, 1)
                elif part in (2, 3):
                    r = part - 2
                    left = (rprob, rest)[r]
                    n = 5 + 4 * r
                    if (b, r) == (0, 0):
                        dve.wait_ge(pool_consts_ready, 1)
                    after(n)
                    dve.tensor_reduce(top[:, r, :], left[:], AX.X, ALU.max).then_inc(route_steps, 1)
                    after(n + 1)
                    dve.tensor_tensor(tie[:, r], left[:], spread(top[:, r, :]), ALU.is_equal).then_inc(tie_ready, 1)
                    dve.wait_ge(tie_ready, 4 * b + 2 * r + 1)
                    dve.tensor_tensor(tie[:, r], tie[:, r], rank[:], ALU.mult).then_inc(tie_ready, 1)
                    dve.wait_ge(tie_ready, 4 * b + 2 * r + 2)
                    dve.tensor_reduce(first[:, r, :], tie[:, r], AX.X, ALU.max).then_inc(route_steps, 1)
                    after(n + 2)
                    dve.tensor_tensor(chosen[:, r], tie[:, r], spread(first[:, r, :]), ALU.is_equal).then_inc(route_steps, 1)
                    after(n + 3)
                    if r == 0:
                        dve.scalar_tensor_tensor(rest[:], chosen[:, 0], -4.0, rprob[:], ALU.mult,
                                                 ALU.add).then_inc(route_steps, 1)
                elif part == 4:
                    dve.tensor_tensor(coef[:, b], chosen[:, 0], chosen[:, 1], ALU.add).then_inc(route_steps, 1)
                    after(13)
                    dve.tensor_tensor(coef[:, b], coef[:, b], rprob[:], ALU.mult).then_inc(route_steps, 1)

            def gate_times_up(i):
                routed = i % PAIRS > 0
                dve.wait_ge(up_filled, i + 1)
                dve.wait_ge(silu_ready, i + 1)
                if i >= 2:
                    dve.wait_ge(act_lo_ready, i - 1)
                dve.tensor_tensor(gated_buf(i) if routed else act_buf(i), silu_buf(i), ps[:, 2 + i % 2, :],
                                  ALU.mult).then_inc(gated_ready, 1)
                if not routed:
                    dve.wait_ge(gated_ready, i + 1)
                    dve.sem_inc(act_ready, 1)

            def times_coef(i):
                unit = ("C", i)
                dve.wait_ge(gated_ready, i + 1)
                wait_ring(dve, ring_filled, None, unit)
                dve.tensor_tensor(act_buf(i), gated_buf(i), bank_of(unit), ALU.mult).then_inc(act_ready, 1)
                dve.wait_ge(act_ready, i + 1)
                dve.sem_inc(ring_done, 1)

            def activation_lo(i):
                hi, lo = act_hl(i)
                dve.wait_ge(act_hi_ready, i + 1)
                dve.tensor_tensor(lo, act_buf(i), hi.bitcast(F32), ALU.subtract).then_inc(act_lo_ready, 1)

            def walk(p, text, n):
                for step in steps(text, n):
                    name, *of = step
                    if name == "S":
                        row_max(p, *of)
                    elif name == "I":
                        invert(p, *of)
                    elif name in "TPRL":
                        take_lo(p, step)
                    elif name == "O":
                        add_out(p, *of)
                    elif name == "W":
                        if of == [0]:
                            modulations()
                        split_weights(*of)
                    elif name == "M":
                        statistics(*of)
                    elif name == "Z":
                        mean_and_variance(*of)
                    elif name == "Y":
                        normalise_rows(*of)
                    elif name == "G":
                        gate_attention(*of)
                    elif name == "F":
                        add_rows(*of, step)
                    elif name == "E":
                        router_logits(*of)
                    elif name == "J":
                        route(*of)
                    elif name == "U":
                        gate_times_up(*of)
                    elif name == "C":
                        times_coef(*of)
                    elif name == "H":
                        activation_lo(*of)
                    elif name == "B":
                        add_rows(*divmod(of[0], NBLK), step)

            all_stages(dve, walk)

        @block.tensor
        def _(pe):
            pe.wait_ge(c_ready, 1)
            for k in range(6):
                ins = pe.matmul(ps[:, RING0, k * B:(k + 1) * B], st_mod[:, k, :], csilu[:], start=(k == 0), stop=(k == 5),
                                skip_group_check=True)
            ins.then_inc(mod_filled, 1)
            pe.wait_ge(vo_loaded, 32)
            for h in range(H):
                ins = pe.matmul(ps[:, h // 4, M * (h % 4):M * (h % 4 + 1)], st_vT[:, h, :], st_o[:, h, :], start=True, stop=True)
            ins.then_inc(wvo_filled, 1)
            pe.wait_ge(ident_loaded, 16)

            def product(dst, left, right, lcols, rcols, first=True, last=True):
                ins = None
                for k, (a, c) in enumerate(((0, 0), (0, 1), (1, 0))):
                    ins = pe.matmul(dst, lcols(left[a]), rcols(right[c]), start=first and k == 0, stop=last and k == 2)
                return ins

            def turn(bank, tiles):
                for j, tile in enumerate(tiles):
                    ins = pe.transpose(bank[:, P * j:P * (j + 1)], tile, ident[:])
                return ins

            def fill(p, unit):
                kind, *of = unit
                bank = bank_of(unit)
                if RI[unit] >= RING:
                    wait_ring(pe, ring_done, p, unit, back=RING)
                if kind == "P":
                    n, t = of
                    if n % H == 0:
                        wait_ring(pe, ring_done, p, ("L", n // H, t // TPB))
                    if n < 2 and t == 0 and p is None:
                        pe.wait_ge(w_ready, n + 1)
                    head = n % H if p is None else 2 * p + n % H
                    ins = product(bank[:, 0:QKV], hT_hl, wqkv, lambda a: a[:, P * t:P * (t + 1)], lambda a: a[:, head, :])
                elif kind == "R":
                    n, k, s = of
                    wait_tile(pe, rotated_ready, p, n, TPB * k + TPB - 1)
                    ins = turn(bank, [rotated[:, t, D * s:D * (s + 1)] for t in range(TPB * k, TPB * (k + 1))])
                elif kind == "T":
                    n, t, u = of
                    wait_tile(pe, probs_ready, p, n, t)
                    ins = turn(bank, [probs[:, t % 4, P * j:P * (j + 1)] for j in range(TPB * u, min(TPB * u + TPB, t + 1))])
                elif kind == "L":
                    i, k = of
                    pe.wait_ge(normed_ready, NBLK * i + k + 1)
                    ins = turn(bank, [normed[:, t, :] for t in range(TPB * k, TPB * (k + 1))])
                elif kind == "F":
                    b, k = of
                    pe.wait_ge(attn_gated, NBLK * b + k + 1)
                    ins = turn(bank, [attnT[:, b, P * t:P * (t + 1)] for t in range(TPB * k, TPB * (k + 1))])
                elif kind == "E":
                    pe.wait_ge(hT_ready, NBLK * (B + of[0] + 1))
                    for t in range(TILES):
                        ins = pe.matmul(bank[:, E * t:E * (t + 1)], hT[:, P * t:P * (t + 1)], router_sb[:], start=(t == 0),
                                        stop=(t == TILES - 1), skip_group_check=True)
                elif kind == "C":
                    c = coef_index(of[0])
                    pe.wait_ge(coef_spread, c + 1)
                    ins = turn(bank, [coef_buf(c)[:, t, :] for t in range(TPB)])
                elif kind == "B":
                    pe.wait_ge(yT_ready, of[0] + 1)
                    ins = turn(bank, [yT(of[0])[:, P * t:P * (t + 1)] for t in range(TPB)])
                ins.then_inc(ring_filled, 1)

            def scores(p, n, t):
                at, pieces = score_cols(t)
                if (n, t) == (0, 0):
                    pe.wait_ge(consts_ready, 1)
                    pe.wait_ge(w_ready, 2)
                if (n, t) >= (0, 2):
                    m = (n, t - 2) if t >= 2 else (n - 1, t + TILES - 2)
                    wait_tile(pe, exp_ready, p, *m)
                if t % TPB == 0:
                    wait_ring(pe, ring_done, p, ("R", n, t // TPB, 1))
                pair = score_pair(t)
                for i, (dst, src, w) in enumerate(pieces):
                    product(pair[:, dst:dst + w], q_hl[n % 2], k_hl[n % 2], lambda a: a[:, P * t:P * (t + 1)],
                            lambda a: a[:, src:src + w], last=(i < len(pieces) - 1))
                end = at + (t + 1) * P
                pe.matmul(pair[:, end - P:end], identb[:], causalb[:], start=False, stop=True).then_inc(scores_filled, 1)

            def attend(p, n, k, j0, j1):
                if j0 == 0:
                    pe.wait_ge(outT_added, pos(p, NBLK * n + k + 1, 2 * NBLK))
                    t = TPB * (k + 1) - 1
                    wait_ring(pe, ring_done, p, ("T", n, t, t // TPB))
                for j in range(j0, j1):
                    c0 = P * max(0, j - TPB * k)
                    ins = product(ps[:, OUT_BANK, c0:BLOCK], v_hl[n % 2], probsT[k], lambda a: a[:, j, :],
                                  lambda a: a[:, j, c0:BLOCK], first=(j == 0), last=(j == TPB * (k + 1) - 1))
                if j1 == TPB * (k + 1):
                    ins.then_inc(outT_filled, 1)

            def gate_and_up(i):
                b, k, g = group(i)
                if i == 0:
                    pe.wait_ge(wffn_ready, 1)
                if i < 2:
                    wait_tile(pe, exp_ready, None, B * H - 1, TILES - 1)
                else:
                    pe.wait_ge(silu_ready, i - 1)
                if i % PAIRS == 0:
                    wait_ring(pe, ring_done, None, ("L", B + b, k))
                hl = norm_hl[B + b]
                product(ps[:, i % 2, :], wgu, hl, lambda a: a[:, 2 * g, :], lambda a: a[:, cols_of(k)]).then_inc(gate_filled, 1)
                if i >= 2:
                    pe.wait_ge(gated_ready, i - 1)
                product(ps[:, 2 + i % 2, :], wgu, hl, lambda a: a[:, 2 * g + 1, :],
                        lambda a: a[:, cols_of(k)]).then_inc(up_filled, 1)

            def down(i):
                j, place = divmod(i, PAIRS)
                g = group(i)[2]
                if place == 0:
                    if j == 0:
                        pe.wait_ge(outT_added, NBLK * B * H + 1)
                    else:
                        pe.wait_ge(yT_ready, j)
                pe.wait_ge(act_lo_ready, i + 1)
                ins = product(ps[:, OUT_BANK, :], wdn, act_hl(i), lambda a: a[:, g, :], lambda a: a,
                              first=(place == 0), last=(place == PAIRS - 1))
                if place == PAIRS - 1:
                    ins.then_inc(y_filled, 1)

            def walk(p, text, n):
                for step in steps(text, n):
                    name, *of = step
                    if name == "S":
                        scores(p, *of)
                    elif name == "A":
                        attend(p, *of)
                    elif name in RING_STEPS:
                        fill(p, step)
                    elif name == "U":
                        gate_and_up(*of)
                    elif name == "D":
                        down(*of)

            all_stages(pe, walk)

_OUT = (2, 1024, 128)


def kernel(**inputs):
    import concourse.bacc as _bacc
    from concourse.bass_utils import run_bass_kernel_spmd as _run

    a = {k: np.asarray(v) for k, v in inputs.items()}
    M, H, D = a["L0_attn_w_aq"].shape
    T = a["L0_attn_x"].shape[1]
    E = a["L0_ffn_router"].shape[1]
    half = D // 2
    freqs = np.power(np.float32(10000.0), -np.arange(half, dtype=np.float32) / np.float32(half)).astype(np.float32)
    radians = (np.arange(T, dtype=np.float32)[:, None] * freqs[None, :]).astype(np.float64)
    cos, sin = np.cos(radians).astype(np.float32), np.sin(radians).astype(np.float32)

    def by_tile(m):
        return m.reshape(T // P, P, m.shape[1]).transpose(1, 0, 2)

    gate, up = a["L0_ffn_experts_gate"], a["L0_ffn_experts_up"]
    pairs = [w for g in range(E // 2) for w in (np.concatenate([gate[2 * g], gate[2 * g + 1]], 1),
                                                np.concatenate([up[2 * g], up[2 * g + 1]], 1))]
    pairs += [a["L0_ffn_shared_gate"], a["L0_ffn_shared_up"]]
    down = a["L0_ffn_experts_down"]
    downs = [np.concatenate([down[2 * g], down[2 * g + 1]], 0) for g in range(E // 2)] + [a["L0_ffn_shared_down"]]
    arrays = {
        "x": a["L0_attn_x"],
        "w_qk": np.concatenate([a["L0_attn_w_aq"], a["L0_attn_w_ak"]], 2),
        "w_vT": a["L0_attn_w_av"].transpose(2, 1, 0),
        "w_o": a["L0_attn_w_ao"].transpose(1, 0, 2),
        "router": a["L0_ffn_router"],
        "w_gate_up": np.stack(pairs, 1),
        "w_down": np.stack(downs, 1),
        "cT": a["L0_c"].T,
        "w_mod": a["L0_wmod"].reshape(M, 6, M),
        "cos_t": by_tile(cos),
        "sin_t": by_tile(np.concatenate([-sin, sin], 1)),
        "causal": np.where(np.arange(P)[None, :] > np.arange(P)[:, None], np.float32(-1e30), np.float32(0)),
        "ident_in": np.eye(P, dtype=np.float32),
    }
    nc = _bacc.Bacc("TRN2", target_bir_lowering=False, num_devices=1)
    fed, aps = {}, []
    for name, arr in arrays.items():
        arr = np.ascontiguousarray(arr)
        fed[f"in_{name}"] = arr
        aps.append(nc.dram_tensor(f"in_{name}", arr.shape, mybir.dt.from_np(arr.dtype), kind="ExternalInput").ap())
    aps.append(nc.dram_tensor("out_dram", _OUT, F32, kind="ExternalOutput").ap())
    build(nc, *aps)
    r = _run(nc, [fed], core_ids=[0])
    return r.results[0]["out_dram"]
```

```python
from contextlib import ExitStack

import numpy as np

import concourse.bass as bass
from concourse import mybir

F32 = mybir.dt.float32
F32R = mybir.dt.float32r
BF16 = mybir.dt.bfloat16
ALU = mybir.AluOpType
ACT = mybir.ActivationFunctionType
AX = mybir.AxisListType

P = 128
RING = 3
B, H = 2, 8
NBLK = 2
PAIRS = 5
GROUPS = B * NBLK * PAIRS
EPS = 1e-5
ROUTE = 13
BLOCK = 512
TPB = BLOCK // P
SHIFT, SCALE, GATE = 0, 1, 2


HEAD_STEPS = "SXINTAOPRr"
STAGE = """
T' 5 0; N' 7; A' 0 0 1; A' 0 1 2; I' 7; T' 6 0; S 0; T' 5 1
X 0; I 0; S 1; T' 6 1; N 0; A' 0 2 3
O' 0; T' 7 0; A' 0 3 4; X 1; N 1; T' 7 1; I 1; S 2
R 1 0; S 3; R 1 1; A' 1 0 2; P+ 0; I 2; A' 1 2 3; N 2; X 2; P+ 1; A' 1 3 4; T 0 0; N 3; X 3; S 4; I 3
T 1 0; X 4; P+ 2; S 5; T 2 0
P+ 3; A' 1 4 5; N 4; S 6; I 4; P+ 4; X 5
A' 1 5 6; N 5; A' 1 6 7; P+ 5; T 3 0; I 5; A' 1 7 8
S 7; X 6; P+ 6; N 6; T 4 0; R+ 0 0; I 6; T 4 1; O' 1; X 7; R+ 0 1; P+ 7
"""
START = """
M 0 0; M 0 1; Z 0; K 0; Y 0 0; W 0; Y 0 1; L 0 0; L 0 1; P+ 0; P+ 1; r+ 0; P+ 2; r+ 1; r+ 2; P+ 3; P+ 4; r+ 3
W 1; P+ 5; R+ 0 0; R+ 0 1; r+ 4; K 1; P+ 6
"""
NEXT = {
    0: {0: "r 5; P 7; W 2", 1: "r 6; r 7; M 1 0", 3: "M 1 1; K 2; Z 1", 4: "K 4; K 3", 6: "Y 1 0; Y 1 1"},
    H - 1: {3: "L 1 0; L 1 1"},
    B * H - 1: {0: "G 0 0; G 0 1", 3: "F 0 0; M 2 0; F 0 1", 4: "M 2 1; Z 2", 5: "Y 2 0; Y 2 1", 6: "L 2 0",
        7: "L 2 1"},
}
LAST = """
E 0; T' 5 0; I' 7; J 0 0; N' 7; J 0 1; A' 0 0 1; T' 6 1; T' 6 0; A' 0 1 2; A' 0 2 4; T' 5 1; T' 7 1; T' 7 0
O' 0; J 0 2; U 0; J 0 3; A' 1 0 8; J 0 4; G 1 0; V 1; V 2; V 3; V 4; O' 1; G 1 1; F 1 0; U 1; H 0; F 1 1; M 3 0
M 3 1; C 1; Z 3
"""
BETWEEN = {3: "Y 3 0; Y 3 1", 4: "L 3 0; L 3 1", 5: "J 1 0; E 1; J 1 1; J 1 2", 9: "J 1 3; J 1 4"}
RING_STEPS = "TPRLFECB"
SPLIT_STEPS = "TPRL"


def stage_text(n):
    slots = STAGE.strip().split("\n")
    return "; ".join((NEXT[n][i] + "; " if i in NEXT.get(n, {}) else "") + slot for i, slot in enumerate(slots))


def expert_text():
    out = []
    for i in range(GROUPS + 3):
        if i < GROUPS:
            out.append(f"U {i}")
            if i % PAIRS:
                out.append(f"C {i}")
                if i + PAIRS < GROUPS:
                    out.append(f"V {i + PAIRS}")
        if 0 <= i - 1 < GROUPS:
            out.append(f"H {i - 1}")
        if 0 <= i - 2 < GROUPS:
            out.append(f"D {i - 2}")
            if (i - 2) % PAIRS == PAIRS - 1:
                out.append(f"Q {(i - 2) // PAIRS}")
        if i >= 3 and (i - 3) % PAIRS == PAIRS - 1:
            out.append(f"B {(i - 3) // PAIRS}")
        if i in BETWEEN:
            out.append(BETWEEN[i])
    begun = LAST.replace("\n", ";").replace("; ", ";").split(";")
    return "; ".join(step for step in out if step not in begun)


def steps(text, n):
    for step in text.replace("\n", ";").split(";"):
        if step.strip():
            name, *rest = step.split()
            rest = tuple(map(int, rest))
            if name[0] not in HEAD_STEPS:
                yield (name[0],) + rest
            else:
                head = n + {"'": -1, "+": 1}.get(name[1:], 0)
                if 0 <= head < B * H:
                    yield (name[0], head) + rest


def ring_plan(kinds):
    texts = [(START, -1)] + [(stage_text(n), n) for n in range(B * H)] + [(LAST, B * H), (expert_text(), None)]
    every = [s for text, n in texts for s in steps(text, n)]
    return {s: i for i, s in enumerate(s for s in every if s[0] in kinds)}


def build(nc, x, w_qk, w_vT, w_o, router, w_gate_up, w_down, cT, w_mod, cos_t, sin_t, causal, ident_in, out):
    _, T, M = x.shape
    D = w_qk.shape[2] // 2
    E = router.shape[1]
    TILES = T // P
    HALF = D // 2
    QKV = 3 * D
    EPAIRS = E // 2
    SM = 1.0 / D
    assert (M, D, TILES, NBLK * BLOCK) == (P, P, 8, T)
    assert (B, H, PAIRS) == (x.shape[0], w_qk.shape[1], w_down.shape[1])
    LOOPED = (H - 2) // 2
    RI = ring_plan(RING_STEPS)
    SPLIT = ring_plan(SPLIT_STEPS)
    PER = RI[("T", 3, 0, 0)] - RI[("T", 1, 0, 0)]
    assert PER % RING == 0

    with ExitStack() as ctx:
        def sb(name, shape, dt=F32):
            return ctx.enter_context(nc.sbuf_tensor(name, shape, dt))

        def sem(name):
            return ctx.enter_context(nc.semaphore(name))

        ps = ctx.enter_context(nc.psum_tensor("ps", [P, 8, BLOCK], F32))
        OUT_BANK, RING0 = 4, 5

        wqkv = [sb(f"wqkv_{s}", [P, H, QKV], F32R) for s in ("hi", "lo")]
        wgu = [sb(f"wgu_{s}", [P, 2 * PAIRS, P], F32R) for s in ("hi", "lo")]
        wdn = [sb(f"wdn_{s}", [P, PAIRS, P], F32R) for s in ("hi", "lo")]
        router_sb = sb("router_sb", [P, E])
        cos_sb = sb("cos_sb", [P, TILES, HALF])
        sin_sb = sb("sin_sb", [P, TILES, D])
        ident = sb("ident", [P, P])
        identb = sb("identb", [P, P], BF16)
        causalb = sb("causalb", [P, P], BF16)
        c_sb = sb("c_sb", [P, B])
        csilu = sb("csilu", [P, B])
        mod_all = sb("mod_all", [P, 6, B])
        mod_sign = sb("mod_sign", [P, 2, B])
        mod_size = sb("mod_size", [P, 2, B])
        rows = sb("rows", [P, B, TILES, M])
        stats = sb("stats", [P, TILES, 6])
        mean_sum = sb("mean_sum", [P, TILES])
        mean_gap = sb("mean_gap", [P, TILES])
        mean = sb("mean", [P, TILES])
        gap2 = sb("gap2", [P, TILES])
        squares = sb("squares", [P, TILES])
        squares2 = sb("squares2", [P, TILES])
        vareps = sb("vareps", [P, TILES])
        minus_half = sb("minus_half", [P, TILES])
        rstd = sb("rstd", [P, TILES])
        normed = sb("normed", [P, TILES, M])
        hT = sb("hT", [P, T])
        hT_hl = [sb(f"hT_{s}", [P, T], F32R) for s in ("hi", "lo")]
        q_hl = [[sb(f"q_{s}{k}", [P, T], F32R) for s in ("hi", "lo")] for k in range(2)]
        k_hl = [[sb(f"k_{s}{k}", [P, T], F32R) for s in ("hi", "lo")] for k in range(2)]
        v_hl = [[sb(f"v_{s}{k}", [P, TILES, M], F32R) for s in ("hi", "lo")] for k in range(2)]
        qk_raw = sb("qk_raw", [P, 2, 2 * D])
        cos_part = sb("cos_part", [P, 2, 2 * D])
        sin_part = sb("sin_part", [P, 2, 2 * D])
        rotated = sb("rotated", [P, TILES, 2 * D])
        probs = sb("probs", [P, 4, T])
        probsT = [[sb(f"probsT{k}_{s}", [P, TPB * (k + 1), BLOCK], F32R) for s in ("hi", "lo")] for k in range(NBLK)]
        neg_max = sb("neg_max", [P, TILES])
        row_sum = sb("row_sum", [P, TILES])
        inv_sum = sb("inv_sum", [P, TILES])
        attnT = sb("attnT", [P, B, T])
        lmax = sb("lmax", [P, TILES])
        lsub = sb("lsub", [P, TILES, E])
        lexp = sb("lexp", [P, TILES, E])
        lsum = sb("lsum", [P, TILES])
        linv = sb("linv", [P, TILES])
        rprob = sb("rprob", [P, TILES, E])
        rank = sb("rank", [P, TILES, E])
        top = sb("top", [P, 2, TILES])
        tie = sb("tie", [P, 2, TILES, E])
        first = sb("first", [P, 2, TILES])
        chosen = sb("chosen", [P, 2, TILES, E])
        rest = sb("rest", [P, TILES, E])
        coef = sb("coef", [P, B, TILES, E])

        st_vT = probs[:, 0, :].rearrange("p (h d) -> p h d", d=D)
        st_o = probs[:, 1, :].rearrange("p (h d) -> p h d", d=M)
        st_mod = hT[:, 0:6 * M].rearrange("p (k d) -> p k d", d=M)
        st_qk = probs[:, 2:4, :].rearrange("p a (h d) -> p (a h) d", d=2 * D)
        st_ffn = attnT[:].rearrange("p b t -> p (b t)")
        st_gu = st_ffn[:, 0:2 * PAIRS * P].rearrange("p (g d) -> p g d", d=P)
        st_dn = st_ffn[:, 2 * PAIRS * P:3 * PAIRS * P].rearrange("p (g d) -> p g d", d=P)
        causal_f = st_ffn[:, 3 * PAIRS * P:3 * PAIRS * P + P]
        def silu_buf(i):
            return probs[:, 0, (i % 2) * BLOCK:(i % 2 + 1) * BLOCK]

        def gated_buf(i):
            return probs[:, 1, (i % 2) * BLOCK:(i % 2 + 1) * BLOCK]

        def act_buf(i):
            return probs[:, 2, (i % 2) * BLOCK:(i % 2 + 1) * BLOCK]

        def act_hl(i):
            return [probsT[1][s][:, i % TILES, :] for s in (0, 1)]

        def coef_buf(i):
            return rotated[:, 2 * (i % 4):2 * (i % 4) + 2, :].rearrange("p a (t d) -> p (a t) d", d=P)

        def yT(j):
            return probs[:, 3, (j % 2) * BLOCK:(j % 2 + 1) * BLOCK]

        norm_hl = [hT_hl, hT_hl, hT_hl, q_hl[0]]

        x_loaded = sem("x_loaded")
        x_last_loaded = sem("x_last_loaded")
        qk_loaded = sem("qk_loaded")
        qk_rest_loaded = sem("qk_rest_loaded")
        vo_loaded = sem("vo_loaded")
        c_loaded = sem("c_loaded")
        mod_loaded = sem("mod_loaded")
        ident_loaded = sem("ident_loaded")
        tables_loaded = sem("tables_loaded")
        ffn_loaded = sem("ffn_loaded")
        pool_consts_ready = sem("pool_consts_ready")
        consts_ready = sem("consts_ready")
        c_ready = sem("c_ready")
        mod_filled = sem("mod_filled")
        mod_steps = sem("mod_steps")
        wvo_filled = sem("wvo_filled")
        w_hi_ready = sem("w_hi_ready")
        w_ready = sem("w_ready")
        w_rest_ready = sem("w_rest_ready")
        wffn_hi_ready = sem("wffn_hi_ready")
        wffn_ready = sem("wffn_ready")
        stats_ready = sem("stats_ready")
        halves_ready = sem("halves_ready")
        var_steps = sem("var_steps")
        pool_waits = sem("pool_waits")
        vareps_ready = sem("vareps_ready")
        rstd_ready = sem("rstd_ready")
        normed_ready = sem("normed_ready")
        hT_ready = sem("hT_ready")
        ring_filled = sem("ring_filled")
        ring_hi_ready = sem("ring_hi_ready")
        ring_done = sem("ring_done")
        sin_ready = sem("sin_ready")
        rotated_ready = sem("rotated_ready")
        scores_filled = sem("scores_filled")
        max_ready = sem("max_ready")
        exp_ready = sem("exp_ready")
        inv_ready = sem("inv_ready")
        probs_ready = sem("probs_ready")
        outT_filled = sem("outT_filled")
        outT_added = sem("outT_added")
        attn_gated = sem("attn_gated")
        route_steps = sem("route_steps")
        route_exp = sem("route_exp")
        tie_ready = sem("tie_ready")
        coef_spread = sem("coef_spread")
        gate_filled = sem("gate_filled")
        up_filled = sem("up_filled")
        silu_ready = sem("silu_ready")
        gated_ready = sem("gated_ready")
        act_hi_ready = sem("act_hi_ready")
        act_lo_ready = sem("act_lo_ready")
        y_filled = sem("y_filled")
        yT_ready = sem("yT_ready")
        stored = sem("stored")

        def pos(p, count, per_pair):
            return count if p is None else count + p * per_pair

        def wait_tile(eng, s, p, n, t):
            eng.wait_ge(s, pos(p, TILES * n + t + 1, 2 * TILES))

        def wait_ring(eng, s, p, unit, back=0):
            order = SPLIT if s is ring_hi_ready else RI
            eng.wait_ge(s, pos(p, order[unit] + 1 - back, PER))

        def bank_of(unit):
            return ps[:, RING0 + RI[unit] % RING, :]

        def tiles_of(k):
            return slice(TPB * k, TPB * (k + 1))

        def cols_of(k):
            return slice(BLOCK * k, BLOCK * (k + 1))

        def group(i):
            j, place = divmod(i, PAIRS)
            return j // NBLK, j % NBLK, (place - 1) % PAIRS

        def coef_index(i):
            return EPAIRS * (i // PAIRS) + i % PAIRS - 1

        def all_stages(eng, walk):
            walk(None, START, -1)
            for b in range(B):
                n = b * H
                walk(None, stage_text(n), n)
                with eng.Fori(0, LOOPED) as p:
                    walk(p, stage_text(n + 1), n + 1)
                    walk(p, stage_text(n + 2), n + 2)
                walk(None, stage_text(n + H - 1), n + H - 1)
            walk(None, LAST, B * H)
            walk(None, expert_text(), None)

        def score_cols(t):
            w = (t + 1) * P
            if w == BLOCK + P:
                return P, [(P, 0, 3 * P), (BLOCK, 3 * P, 2 * P)]
            return 0, [(c, c, min(BLOCK, w - c)) for c in range(0, w, BLOCK)]

        def score_pair(t):
            return ps[:, 2 * (t % 2):2 * (t % 2) + 2, :].rearrange("p a c -> p (a c)")

        def view(ap, dims, offset=0):
            return bass.AP(ap.tensor, ap.offset + offset, [ap.ap[0]] + dims)

        block = ctx.enter_context(nc.Block())

        @block.sync
        def _(sp):
            sp.dma_start(rows[:, 0], x[0].rearrange("(t p) m -> p t m", p=P)).then_inc(x_loaded, 16)
            sp.dma_start(c_sb[:], cT).then_inc(c_loaded, 16)
            sp.dma_start(ident[:], ident_in).then_inc(ident_loaded, 16)
            sp.dma_start(st_qk[:, 0:1, :], w_qk[:, 0:1, :]).then_inc(qk_loaded, 16)
            sp.dma_start(cos_sb[:], cos_t).then_inc(tables_loaded, 16)
            sp.dma_start(sin_sb[:], sin_t).then_inc(tables_loaded, 16)
            sp.dma_start(causal_f, causal).then_inc(tables_loaded, 16)
            sp.dma_start(st_qk[:, 1:H, :], w_qk[:, 1:H, :]).then_inc(qk_rest_loaded, 16)
            sp.dma_start(rows[:, 1], x[1].rearrange("(t p) m -> p t m", p=P)).then_inc(x_last_loaded, 16)
            for j in range(B * NBLK):
                b, k = divmod(j, NBLK)
                wait_ring(sp, ring_done, None, ("B", j))
                sp.dma_start(out[b].rearrange("(k t p) m -> k p t m", p=P, t=TPB)[k],
                             rows[:, b, tiles_of(k), :]).then_inc(stored, 16)
            sp.wait_ge(stored, 16 * B * NBLK)

        @block.gpsimd
        def _(pool):
            pool.memset(minus_half[:], -0.5)
            for e in range(E):
                ins = pool.memset(rank[:, :, e], float(E - e))
            ins.then_inc(pool_consts_ready, 1)
            pool.dma_start(st_vT, w_vT).then_inc(vo_loaded, 16)
            pool.dma_start(st_o, w_o).then_inc(vo_loaded, 16)
            pool.dma_start(st_gu, w_gate_up).then_inc(ffn_loaded, 16)
            pool.dma_start(st_dn, w_down).then_inc(ffn_loaded, 16)
            pool.dma_start(router_sb[:], router).then_inc(ffn_loaded, 16)

            def zero_sums():
                pool.wait_ge(wffn_ready, 1)
                pool.wait_ge(consts_ready, 1)
                pool.memset(attnT[:], 0.0).then_inc(outT_added, 1)

            def split_rest():
                pool.wait_ge(w_hi_ready, 4)
                pool.tensor_tensor(wqkv[1][:, 1:H, 0:2 * D], st_qk[:, 1:H, :], wqkv[0][:, 1:H, 0:2 * D].bitcast(F32),
                                   ALU.subtract).then_inc(w_rest_ready, 1)

            def rstd_step(i):
                if i == 0:
                    pool.wait_ge(pool_consts_ready, 1)
                pool.wait_ge(vareps_ready, i + 1)
                pool.tensor_tensor(rstd[:], vareps[:], minus_half[:], ALU.pow).then_inc(rstd_ready, 1)

            def rotate(p, n, t):
                unit = ("P", n, t)
                by_dve = n == 0 and p is None
                if by_dve and t >= 2:
                    wait_tile(pool, rotated_ready, p, n, t - 2)
                if (n, t) == (1, 0) and p is None:
                    wait_tile(pool, rotated_ready, p, 0, TILES - 1)
                if (n, t) == (0, 0):
                    pool.wait_ge(tables_loaded, 48)
                raw = qk_raw[:, t % 2, :]
                swapped = view(raw, [[D, 2], [-HALF, 2], [1, HALF]], HALF)
                wait_ring(pool, ring_hi_ready, p, unit)
                pool.tensor_tensor(view(sin_part[:, t % 2, :], [[D, 2], [HALF, 2], [1, HALF]]), swapped,
                                   view(sin_sb[:, t, :], [[0, 2], [HALF, 2], [1, HALF]]), ALU.mult).then_inc(sin_ready, 1)
                if by_dve:
                    return
                wait_tile(pool, sin_ready, p, n, t)
                wait_ring(pool, ring_done, p, unit)
                pool.tensor_tensor(rotated[:, t, :], cos_part[:, t % 2, :], sin_part[:, t % 2, :],
                                   ALU.add).then_inc(rotated_ready, 1)

            def normalise(p, n, t):
                w = (t + 1) * P
                wait_tile(pool, inv_ready, p, n, t)
                pool.sem_inc(pool_waits, 1)
                pool.tensor_scalar(probs[:, t % 4, 0:w], probs[:, t % 4, 0:w], inv_sum[:, t:t + 1], 1.0,
                                   ALU.mult, ALU.mult).then_inc(probs_ready, 1)

            def spread_coef(i):
                b, k, g = group(i)
                c = coef_index(i)
                pool.wait_ge(route_steps, ROUTE * (b + 1))
                if c >= EPAIRS:
                    wait_ring(pool, ring_filled, None, ("C", i - PAIRS))
                pool.sem_inc(pool_waits, 1)
                pool.tensor_scalar(coef_buf(c).rearrange("p t (e d) -> p t e d", e=2),
                                   view(coef[:, b, TPB * k, 2 * g:2 * g + 2], [[E, TPB], [1, 2], [0, P // 2]]),
                                   1.0, 1.0, ALU.mult, ALU.mult).then_inc(coef_spread, 1)

            def walk(p, text, n):
                for step in steps(text, n):
                    name, *of = step
                    if name == "N":
                        normalise(p, *of)
                    elif name == "P":
                        rotate(p, *of)
                    elif step == ("K", 4):
                        zero_sums()
                    elif step == ("W", 2):
                        split_rest()
                    elif name == "Z":
                        rstd_step(*of)
                    elif name == "V":
                        spread_coef(*of)

            all_stages(pool, walk)

        @block.scalar
        def _(act):
            act.dma_start(st_mod, w_mod).then_inc(mod_loaded, 16)
            act.wait_ge(c_loaded, 16)
            act.activation(csilu[:], c_sb[:], ACT.Silu).then_inc(c_ready, 1)

            def split_weights(s):
                if s != 1:
                    heads = slice(0, 1) if s == 0 else slice(1, H)
                    act.wait_ge(qk_loaded if s == 0 else qk_rest_loaded, 16)
                    act.copy(wqkv[0][:, heads, 0:2 * D], st_qk[:, heads, :]).then_inc(w_hi_ready, 1)
                if s != 2:
                    heads = slice(0, 1) if s == 0 else slice(1, H)
                    wvo = ps[:, 0:2, :].rearrange("p a (h m) -> p (a h) m", m=M)
                    act.wait_ge(wvo_filled, s + 1)
                    act.copy(wqkv[0][:, heads, 2 * D:QKV], wvo[:, heads, :]).then_inc(w_hi_ready, 1)

            def constants():
                act.wait_ge(ident_loaded, 16)
                act.wait_ge(tables_loaded, 48)
                act.copy(identb[:], ident[:])
                act.activation(lexp[:, 0, 0:1], ident[:, 0:1], ACT.Exp)
                act.copy(causalb[:], causal_f).then_inc(consts_ready, 1)

            def experts_hi():
                act.wait_ge(ffn_loaded, 48)
                act.copy(wgu[0][:], st_gu)
                act.copy(wdn[0][:], st_dn).then_inc(wffn_hi_ready, 1)

            def modulate(i, k):
                which, b = divmod(i, B)
                unit = ("L", i, k)
                wait_ring(act, ring_filled, None, unit)
                if (i, k) == (0, 0):
                    act.wait_ge(mod_steps, 6)
                act.activation(hT[:, cols_of(k)], bank_of(unit), ACT.Identity,
                               bias=mod_all[:, 3 * which + SHIFT, b:b + 1],
                               scale=mod_all[:, 3 * which + SCALE, b:b + 1]).then_inc(hT_ready, 1)
                act.wait_ge(hT_ready, NBLK * i + k + 1)
                act.copy(norm_hl[i][0][:, cols_of(k)], hT[:, cols_of(k)]).then_inc(ring_hi_ready, 1)

            def exponent(p, n, t):
                at, _ = score_cols(t)
                w = (t + 1) * P
                wait_tile(act, max_ready, p, n, t)
                act.activation(probs[:, t % 4, 0:w], score_pair(t)[:, at:at + w], ACT.Exp, bias=neg_max[:, t:t + 1],
                               accum_out=row_sum[:, t:t + 1]).then_inc(exp_ready, 1)

            def take_hi(p, unit):
                kind, n, t = unit[:3]
                bank = bank_of(unit)
                if kind == "P":
                    if (n, t) >= (0, 2):
                        m = (n, t - 2) if t >= 2 else (n - 1, t + TILES - 2)
                        wait_tile(act, sin_ready, p, *m)
                    wait_ring(act, ring_filled, p, unit)
                    act.copy(qk_raw[:, t % 2, :], bank[:, 0:2 * D])
                    act.copy(v_hl[n % 2][0][:, t, :], bank[:, 2 * D:QKV]).then_inc(ring_hi_ready, 1)
                elif kind == "R":
                    wait_ring(act, ring_filled, p, unit)
                    act.activation((q_hl, k_hl)[unit[3]][n % 2][0][:, cols_of(t)], bank, ACT.Copy,
                                   scale=(SM, 1.0)[unit[3]]).then_inc(ring_hi_ready, 1)
                else:
                    j0 = TPB * unit[3]
                    k = min(TPB, t + 1 - j0)
                    wait_ring(act, ring_filled, p, unit)
                    act.copy(probsT[t // TPB][0][:, j0:j0 + k, P * (t % TPB):P * (t % TPB + 1)],
                             bank[:, 0:k * P].rearrange("p (j i) -> p j i", i=P)).then_inc(ring_hi_ready, 1)

            def route_exponent(b):
                wait_ring(act, ring_done, None, ("E", b))
                act.activation(lexp[:], lsub[:], ACT.Exp).then_inc(route_exp, 1)

            def silu(i):
                act.wait_ge(gate_filled, i + 1)
                if i >= 2:
                    act.wait_ge(gated_ready, i - 1)
                act.activation(silu_buf(i), ps[:, i % 2, :], ACT.Silu).then_inc(silu_ready, 1)

            def activation_hi(i):
                if i % PAIRS:
                    wait_ring(act, ring_done, None, ("C", i))
                else:
                    act.wait_ge(gated_ready, i + 1)
                act.copy(act_hl(i)[0], act_buf(i)).then_inc(act_hi_ready, 1)

            def gate_output(j):
                act.wait_ge(y_filled, j + 1)
                act.activation(yT(j), ps[:, OUT_BANK, :], ACT.Copy,
                               scale=mod_all[:, 3 + GATE, j // NBLK:j // NBLK + 1]).then_inc(yT_ready, 1)

            def walk(p, text, n):
                for step in steps(text, n):
                    name, *of = step
                    if name == "X":
                        exponent(p, *of)
                    elif name in "TPR":
                        take_hi(p, step)
                    elif name == "W":
                        split_weights(*of)
                    elif step == ("K", 1):
                        constants()
                    elif step == ("K", 2):
                        experts_hi()
                    elif name == "L":
                        modulate(*of)
                    elif name == "J" and of[1] == 0:
                        route_exponent(of[0])
                    elif name == "U":
                        silu(*of)
                    elif name == "H":
                        activation_hi(*of)
                    elif name == "Q":
                        gate_output(*of)

            all_stages(act, walk)

        @block.vector
        def _(dve):
            def modulations():
                dve.wait_ge(mod_filled, 1)
                dve.tensor_copy(mod_all[:], ps[:, RING0, 0:6 * B].rearrange("p (k b) -> p k b", b=B)).then_inc(mod_steps, 1)
                dve.wait_ge(mod_steps, 1)
                scales = view(mod_all[:], [[3 * B, 2], [1, B]], SCALE * B)
                gates = view(mod_all[:], [[3 * B, 2], [1, B]], GATE * B)
                dve.tensor_scalar(scales, scales, 1.0, None, ALU.add).then_inc(mod_steps, 1)
                dve.tensor_scalar(mod_sign[:], gates, 0.0, 2.0, ALU.is_ge, ALU.mult).then_inc(mod_steps, 1)
                dve.scalar_tensor_tensor(mod_size[:], gates, -1.0, gates, ALU.mult, ALU.max).then_inc(mod_steps, 1)
                dve.wait_ge(mod_steps, 4)
                dve.tensor_scalar(mod_sign[:], mod_sign[:], -1.0, None, ALU.add).then_inc(mod_steps, 1)
                dve.wait_ge(mod_steps, 5)
                dve.scalar_tensor_tensor(gates, mod_size[:], 0.25, mod_sign[:], ALU.max, ALU.mult).then_inc(mod_steps, 1)

            def split_weights(s):
                heads = slice(0, 1) if s == 0 else slice(1, H)
                wvo = ps[:, 0:2, :].rearrange("p a (h m) -> p (a h) m", m=M)
                dve.wait_ge(w_hi_ready, s + 2)
                if s == 0:
                    dve.tensor_tensor(wqkv[1][:, heads, 0:2 * D], st_qk[:, heads, :],
                                      wqkv[0][:, heads, 0:2 * D].bitcast(F32), ALU.subtract)
                dve.tensor_tensor(wqkv[1][:, heads, 2 * D:QKV], wvo[:, heads, :],
                                  wqkv[0][:, heads, 2 * D:QKV].bitcast(F32), ALU.subtract).then_inc(w_ready, 1)

            def experts_lo():
                dve.wait_ge(wffn_hi_ready, 1)
                dve.tensor_tensor(wgu[1][:], st_gu, wgu[0][:].bitcast(F32), ALU.subtract)
                dve.tensor_tensor(wdn[1][:], st_dn, wdn[0][:].bitcast(F32), ALU.subtract).then_inc(wffn_ready, 1)

            def statistics(i, k):
                which, b = divmod(i, B)
                if k == 0 and which == 0:
                    dve.wait_ge((x_loaded, x_last_loaded)[b], 16)
                if which == 1:
                    wait_ring(dve, ring_done, None, ("F", b, k))
                for t in range(TPB * k, TPB * (k + 1)):
                    ins = dve.bn_stats(stats[:, t, :], rows[:, b, t, :])
                ins.then_inc(stats_ready, 1)

            def mean_and_variance(i):
                dve.wait_ge(stats_ready, NBLK * (i + 1))
                dve.tensor_tensor(mean_sum[:], stats[:, :, 1], stats[:, :, 4], ALU.add)
                dve.tensor_tensor(mean_gap[:], stats[:, :, 1], stats[:, :, 4], ALU.subtract)
                dve.tensor_tensor(squares[:], stats[:, :, 2], stats[:, :, 5], ALU.add).then_inc(halves_ready, 1)
                dve.wait_ge(halves_ready, i + 1)
                dve.tensor_scalar(mean[:], mean_sum[:], 0.5, None, ALU.mult)
                dve.scalar_tensor_tensor(gap2[:], mean_gap[:], 0.25, mean_gap[:], ALU.mult, ALU.mult)
                dve.tensor_scalar(squares2[:], squares[:], 1.0 / M, EPS, ALU.mult, ALU.add).then_inc(var_steps, 1)
                dve.wait_ge(var_steps, i + 1)
                dve.tensor_tensor(vareps[:], gap2[:], squares2[:], ALU.add).then_inc(vareps_ready, 1)

            def normalise_rows(i, k):
                b = i % B
                dve.wait_ge(rstd_ready, i + 1)
                for t in range(TPB * k, TPB * (k + 1)):
                    ins = dve.tensor_scalar(normed[:, t, :], rows[:, b, t, :], mean[:, t:t + 1], rstd[:, t:t + 1],
                                            ALU.subtract, ALU.mult)
                ins.then_inc(normed_ready, 1)

            def row_max(p, n, t):
                at, _ = score_cols(t)
                wait_tile(dve, scores_filled, p, n, t)
                dve.tensor_reduce(neg_max[:, t:t + 1], score_pair(t)[:, at:at + (t + 1) * P], AX.X, ALU.max,
                                  negate=True).then_inc(max_ready, 1)

            def invert(p, n, t):
                wait_tile(dve, exp_ready, p, n, t)
                dve.reciprocal(inv_sum[:, t:t + 1], row_sum[:, t:t + 1]).then_inc(inv_ready, 1)

            def take_lo(p, unit):
                kind, n, t = unit[:3]
                bank = bank_of(unit)
                if kind == "P":
                    if (n, t) == (0, 0):
                        dve.wait_ge(tables_loaded, 48)
                    if (n, t) >= (0, 2):
                        m = (n, t - 2) if t >= 2 else (n - 1, t + TILES - 2)
                        wait_tile(dve, rotated_ready, p, *m)
                    wait_ring(dve, ring_hi_ready, p, unit)
                    dve.tensor_tensor(view(cos_part[:, t % 2, :], [[HALF, 4], [1, HALF]]), view(bank, [[HALF, 4], [1, HALF]]),
                                      view(cos_sb[:, t, :], [[0, 4], [1, HALF]]), ALU.mult)
                    dve.tensor_tensor(v_hl[n % 2][1][:, t, :], bank[:, 2 * D:QKV], v_hl[n % 2][0][:, t, :].bitcast(F32),
                                      ALU.subtract).then_inc(ring_done, 1)
                elif kind == "R":
                    hi, lo = ((q_hl, k_hl)[unit[3]][n % 2][s][:, cols_of(t)] for s in (0, 1))
                    wait_ring(dve, ring_hi_ready, p, unit)
                    dve.scalar_tensor_tensor(lo, bank, (SM, 1.0)[unit[3]], hi.bitcast(F32), ALU.mult,
                                             ALU.subtract).then_inc(ring_done, 1)
                elif kind == "L":
                    hi, lo = (part[:, cols_of(t)] for part in norm_hl[n])
                    wait_ring(dve, ring_hi_ready, None, unit)
                    dve.tensor_tensor(lo, hT[:, cols_of(t)], hi.bitcast(F32), ALU.subtract).then_inc(ring_done, 1)
                else:
                    j0 = TPB * unit[3]
                    k = min(TPB, t + 1 - j0)
                    hi, lo = (probsT[t // TPB][s][:, j0:j0 + k, P * (t % TPB):P * (t % TPB + 1)] for s in (0, 1))
                    wait_ring(dve, ring_hi_ready, p, unit)
                    dve.tensor_tensor(lo, bank[:, 0:k * P].rearrange("p (j i) -> p j i", i=P), hi.bitcast(F32),
                                      ALU.subtract).then_inc(ring_done, 1)

            def add_rotated(n, t):
                wait_tile(dve, sin_ready, None, n, t)
                wait_ring(dve, ring_done, None, ("P", n, t))
                dve.tensor_tensor(rotated[:, t, :], cos_part[:, t % 2, :], sin_part[:, t % 2, :],
                                  ALU.add).then_inc(rotated_ready, 1)

            def add_out(p, n, k):
                part = attnT[:, n // H, cols_of(k)]
                dve.wait_ge(outT_filled, pos(p, NBLK * n + k + 1, 2 * NBLK))
                dve.tensor_tensor(part, part, ps[:, OUT_BANK, :], ALU.add).then_inc(outT_added, 1)

            def gate_attention(b, k):
                part = attnT[:, b, cols_of(k)]
                dve.wait_ge(outT_added, NBLK * (H * b + H - 1) + k + 2)
                dve.tensor_scalar(part, part, mod_all[:, GATE, b:b + 1], None, ALU.mult).then_inc(attn_gated, 1)

            def add_rows(b, k, unit):
                part = rows[:, b, tiles_of(k), :]
                wait_ring(dve, ring_filled, None, unit)
                dve.tensor_tensor(part, bank_of(unit).rearrange("p (t m) -> p t m", m=M), part, ALU.add).then_inc(ring_done, 1)

            def spread(a):
                return view(a, [[1, TILES], [0, E]])

            def router_logits(b):
                unit = ("E", b)
                logits = bank_of(unit)[:, 0:TILES * E].rearrange("p (t e) -> p t e", e=E)
                wait_ring(dve, ring_filled, None, unit)
                dve.tensor_reduce(lmax[:], logits, AX.X, ALU.max).then_inc(route_steps, 1)
                dve.wait_ge(route_steps, ROUTE * b + 1)
                dve.tensor_tensor(lsub[:], logits, spread(lmax[:]), ALU.subtract).then_inc(ring_done, 1)

            def route(b, part):
                def after(n):
                    dve.wait_ge(route_steps, ROUTE * b + n)

                if part == 1:
                    dve.wait_ge(route_exp, b + 1)
                    dve.tensor_reduce(lsum[:], lexp[:], AX.X, ALU.add).then_inc(route_steps, 1)
                    after(2)
                    dve.reciprocal(linv[:], lsum[:]).then_inc(route_steps, 1)
                    after(3)
                    dve.tensor_tensor(rprob[:], lexp[:], spread(linv[:]), ALU.mult).then_inc(route_steps, 1)
                elif part in (2, 3):
                    r = part - 2
                    left = (rprob, rest)[r]
                    n = 4 + 4 * r
                    if (b, r) == (0, 0):
                        dve.wait_ge(pool_consts_ready, 1)
                    after(n)
                    dve.tensor_reduce(top[:, r, :], left[:], AX.X, ALU.max).then_inc(route_steps, 1)
                    after(n + 1)
                    dve.tensor_tensor(tie[:, r], left[:], spread(top[:, r, :]), ALU.is_equal).then_inc(tie_ready, 1)
                    dve.wait_ge(tie_ready, 4 * b + 2 * r + 1)
                    dve.tensor_tensor(tie[:, r], tie[:, r], rank[:], ALU.mult).then_inc(tie_ready, 1)
                    dve.wait_ge(tie_ready, 4 * b + 2 * r + 2)
                    dve.tensor_reduce(first[:, r, :], tie[:, r], AX.X, ALU.max).then_inc(route_steps, 1)
                    after(n + 2)
                    dve.tensor_tensor(chosen[:, r], tie[:, r], spread(first[:, r, :]), ALU.is_equal).then_inc(route_steps, 1)
                    after(n + 3)
                    if r == 0:
                        dve.scalar_tensor_tensor(rest[:], chosen[:, 0], -4.0, rprob[:], ALU.mult,
                                                 ALU.add).then_inc(route_steps, 1)
                elif part == 4:
                    dve.tensor_tensor(coef[:, b], chosen[:, 0], chosen[:, 1], ALU.add).then_inc(route_steps, 1)
                    after(12)
                    dve.tensor_tensor(coef[:, b], coef[:, b], rprob[:], ALU.mult).then_inc(route_steps, 1)

            def gate_times_up(i):
                routed = i % PAIRS > 0
                dve.wait_ge(up_filled, i + 1)
                dve.wait_ge(silu_ready, i + 1)
                if i >= 2:
                    dve.wait_ge(act_lo_ready, i - 1)
                dve.tensor_tensor(gated_buf(i) if routed else act_buf(i), silu_buf(i), ps[:, 2 + i % 2, :],
                                  ALU.mult).then_inc(gated_ready, 1)

            def times_coef(i):
                unit = ("C", i)
                dve.wait_ge(gated_ready, i + 1)
                wait_ring(dve, ring_filled, None, unit)
                dve.tensor_tensor(act_buf(i), gated_buf(i), bank_of(unit), ALU.mult).then_inc(ring_done, 1)

            def activation_lo(i):
                hi, lo = act_hl(i)
                dve.wait_ge(act_hi_ready, i + 1)
                dve.tensor_tensor(lo, act_buf(i), hi.bitcast(F32), ALU.subtract).then_inc(act_lo_ready, 1)

            def walk(p, text, n):
                for step in steps(text, n):
                    name, *of = step
                    if name == "S":
                        row_max(p, *of)
                    elif name == "I":
                        invert(p, *of)
                    elif name in "TPRL":
                        take_lo(p, step)
                    elif name == "r":
                        add_rotated(*of)
                    elif name == "O":
                        add_out(p, *of)
                    elif name == "W" and of[0] < 2:
                        split_weights(*of)
                    elif step == ("K", 0):
                        modulations()
                    elif step == ("K", 3):
                        experts_lo()
                    elif name == "M":
                        statistics(*of)
                    elif name == "Z":
                        mean_and_variance(*of)
                    elif name == "Y":
                        normalise_rows(*of)
                    elif name == "G":
                        gate_attention(*of)
                    elif name == "F":
                        add_rows(*of, step)
                    elif name == "E":
                        router_logits(*of)
                    elif name == "J":
                        route(*of)
                    elif name == "U":
                        gate_times_up(*of)
                    elif name == "C":
                        times_coef(*of)
                    elif name == "H":
                        activation_lo(*of)
                    elif name == "B":
                        add_rows(*divmod(of[0], NBLK), step)

            all_stages(dve, walk)

        @block.tensor
        def _(pe):
            pe.wait_ge(c_ready, 1)
            pe.wait_ge(mod_loaded, 16)
            for k in range(6):
                ins = pe.matmul(ps[:, RING0, k * B:(k + 1) * B], st_mod[:, k, :], csilu[:], start=(k == 0), stop=(k == 5),
                                skip_group_check=True)
            ins.then_inc(mod_filled, 1)
            pe.wait_ge(ident_loaded, 16)

            def product(dst, left, right, lcols, rcols, first=True, last=True):
                ins = None
                for k, (a, c) in enumerate(((0, 0), (0, 1), (1, 0))):
                    ins = pe.matmul(dst, lcols(left[a]), rcols(right[c]), start=first and k == 0, stop=last and k == 2)
                return ins

            def value_output(heads):
                pe.wait_ge(vo_loaded, 32)
                for h in heads:
                    ins = pe.matmul(ps[:, h // 4, M * (h % 4):M * (h % 4 + 1)], st_vT[:, h, :], st_o[:, h, :], start=True,
                                    stop=True)
                ins.then_inc(wvo_filled, 1)

            def turn(bank, tiles):
                for j, tile in enumerate(tiles):
                    ins = pe.transpose(bank[:, P * j:P * (j + 1)], tile, ident[:])
                return ins

            def fill(p, unit):
                kind, *of = unit
                bank = bank_of(unit)
                if RI[unit] >= RING:
                    wait_ring(pe, ring_done, p, unit, back=RING)
                if kind == "P":
                    n, t = of
                    if n % H == 0:
                        wait_ring(pe, ring_done, p, ("L", n // H, t // TPB))
                    if n < 2 and t == 0 and p is None:
                        pe.wait_ge((w_ready, w_rest_ready)[n], 1)
                    head = n % H if p is None else 2 * p + n % H
                    ins = product(bank[:, 0:QKV], hT_hl, wqkv, lambda a: a[:, P * t:P * (t + 1)], lambda a: a[:, head, :])
                elif kind == "R":
                    n, k, s = of
                    wait_tile(pe, rotated_ready, p, n, TPB * k + TPB - 1)
                    ins = turn(bank, [rotated[:, t, D * s:D * (s + 1)] for t in range(TPB * k, TPB * (k + 1))])
                elif kind == "T":
                    n, t, u = of
                    wait_tile(pe, probs_ready, p, n, t)
                    ins = turn(bank, [probs[:, t % 4, P * j:P * (j + 1)] for j in range(TPB * u, min(TPB * u + TPB, t + 1))])
                elif kind == "L":
                    i, k = of
                    pe.wait_ge(normed_ready, NBLK * i + k + 1)
                    ins = turn(bank, [normed[:, t, :] for t in range(TPB * k, TPB * (k + 1))])
                elif kind == "F":
                    b, k = of
                    pe.wait_ge(attn_gated, NBLK * b + k + 1)
                    ins = turn(bank, [attnT[:, b, P * t:P * (t + 1)] for t in range(TPB * k, TPB * (k + 1))])
                elif kind == "E":
                    pe.wait_ge(hT_ready, NBLK * (B + of[0] + 1))
                    for t in range(TILES):
                        ins = pe.matmul(bank[:, E * t:E * (t + 1)], hT[:, P * t:P * (t + 1)], router_sb[:], start=(t == 0),
                                        stop=(t == TILES - 1), skip_group_check=True)
                elif kind == "C":
                    c = coef_index(of[0])
                    pe.wait_ge(coef_spread, c + 1)
                    ins = turn(bank, [coef_buf(c)[:, t, :] for t in range(TPB)])
                elif kind == "B":
                    pe.wait_ge(yT_ready, of[0] + 1)
                    ins = turn(bank, [yT(of[0])[:, P * t:P * (t + 1)] for t in range(TPB)])
                ins.then_inc(ring_filled, 1)

            def scores(p, n, t):
                at, pieces = score_cols(t)
                if (n, t) == (0, 0):
                    pe.wait_ge(consts_ready, 1)
                    pe.wait_ge(w_ready, 2)
                if (n, t) >= (0, 2):
                    m = (n, t - 2) if t >= 2 else (n - 1, t + TILES - 2)
                    wait_tile(pe, exp_ready, p, *m)
                if t % TPB == 0:
                    wait_ring(pe, ring_done, p, ("R", n, t // TPB, 1))
                pair = score_pair(t)
                for i, (dst, src, w) in enumerate(pieces):
                    product(pair[:, dst:dst + w], q_hl[n % 2], k_hl[n % 2], lambda a: a[:, P * t:P * (t + 1)],
                            lambda a: a[:, src:src + w], last=(i < len(pieces) - 1))
                end = at + (t + 1) * P
                pe.matmul(pair[:, end - P:end], identb[:], causalb[:], start=False, stop=True).then_inc(scores_filled, 1)

            def attend(p, n, k, j0, j1):
                if j0 == 0:
                    pe.wait_ge(outT_added, pos(p, NBLK * n + k + 1, 2 * NBLK))
                    t = TPB * (k + 1) - 1
                    wait_ring(pe, ring_done, p, ("T", n, t, t // TPB))
                for j in range(j0, j1):
                    c0 = P * max(0, j - TPB * k)
                    ins = product(ps[:, OUT_BANK, c0:BLOCK], v_hl[n % 2], probsT[k], lambda a: a[:, j, :],
                                  lambda a: a[:, j, c0:BLOCK], first=(j == 0), last=(j == TPB * (k + 1) - 1))
                if j1 == TPB * (k + 1):
                    ins.then_inc(outT_filled, 1)

            def gate_and_up(i):
                b, k, g = group(i)
                if i == 0:
                    pe.wait_ge(wffn_ready, 1)
                if i < 2:
                    wait_tile(pe, exp_ready, None, B * H - 1, TILES - 1)
                else:
                    pe.wait_ge(silu_ready, i - 1)
                if i % PAIRS == 0:
                    wait_ring(pe, ring_done, None, ("L", B + b, k))
                hl = norm_hl[B + b]
                product(ps[:, i % 2, :], wgu, hl, lambda a: a[:, 2 * g, :], lambda a: a[:, cols_of(k)]).then_inc(gate_filled, 1)
                if i >= 2:
                    pe.wait_ge(gated_ready, i - 1)
                product(ps[:, 2 + i % 2, :], wgu, hl, lambda a: a[:, 2 * g + 1, :],
                        lambda a: a[:, cols_of(k)]).then_inc(up_filled, 1)

            def down(i):
                j, place = divmod(i, PAIRS)
                g = group(i)[2]
                if place == 0:
                    if j == 0:
                        pe.wait_ge(outT_added, NBLK * B * H + 1)
                    else:
                        pe.wait_ge(yT_ready, j)
                pe.wait_ge(act_lo_ready, i + 1)
                ins = product(ps[:, OUT_BANK, :], wdn, act_hl(i), lambda a: a[:, g, :], lambda a: a,
                              first=(place == 0), last=(place == PAIRS - 1))
                if place == PAIRS - 1:
                    ins.then_inc(y_filled, 1)

            def walk(p, text, n):
                for step in steps(text, n):
                    name, *of = step
                    if name == "S":
                        scores(p, *of)
                    elif name == "A":
                        attend(p, *of)
                    elif name in RING_STEPS:
                        fill(p, step)
                    elif name == "W" and of[0] < 2:
                        value_output((range(0, 1), range(1, H))[of[0]])
                    elif name == "U":
                        gate_and_up(*of)
                    elif name == "D":
                        down(*of)

            all_stages(pe, walk)

_OUT = (2, 1024, 128)


def kernel(**inputs):
    import concourse.bacc as _bacc
    from concourse.bass_utils import run_bass_kernel_spmd as _run

    a = {k: np.asarray(v) for k, v in inputs.items()}
    M, H, D = a["L0_attn_w_aq"].shape
    T = a["L0_attn_x"].shape[1]
    E = a["L0_ffn_router"].shape[1]
    half = D // 2
    freqs = np.power(np.float32(10000.0), -np.arange(half, dtype=np.float32) / np.float32(half)).astype(np.float32)
    radians = (np.arange(T, dtype=np.float32)[:, None] * freqs[None, :]).astype(np.float64)
    cos, sin = np.cos(radians).astype(np.float32), np.sin(radians).astype(np.float32)

    def by_tile(m):
        return m.reshape(T // P, P, m.shape[1]).transpose(1, 0, 2)

    gate, up = a["L0_ffn_experts_gate"], a["L0_ffn_experts_up"]
    pairs = [w for g in range(E // 2) for w in (np.concatenate([gate[2 * g], gate[2 * g + 1]], 1),
                                                np.concatenate([up[2 * g], up[2 * g + 1]], 1))]
    pairs += [a["L0_ffn_shared_gate"], a["L0_ffn_shared_up"]]
    down = a["L0_ffn_experts_down"]
    downs = [np.concatenate([down[2 * g], down[2 * g + 1]], 0) for g in range(E // 2)] + [a["L0_ffn_shared_down"]]
    arrays = {
        "x": a["L0_attn_x"],
        "w_qk": np.concatenate([a["L0_attn_w_aq"], a["L0_attn_w_ak"]], 2),
        "w_vT": a["L0_attn_w_av"].transpose(2, 1, 0),
        "w_o": a["L0_attn_w_ao"].transpose(1, 0, 2),
        "router": a["L0_ffn_router"],
        "w_gate_up": np.stack(pairs, 1),
        "w_down": np.stack(downs, 1),
        "cT": a["L0_c"].T,
        "w_mod": a["L0_wmod"].reshape(M, 6, M),
        "cos_t": by_tile(cos),
        "sin_t": by_tile(np.concatenate([-sin, sin], 1)),
        "causal": np.where(np.arange(P)[None, :] > np.arange(P)[:, None], np.float32(-1e30), np.float32(0)),
        "ident_in": np.eye(P, dtype=np.float32),
    }
    nc = _bacc.Bacc("TRN2", target_bir_lowering=False, num_devices=1)
    fed, aps = {}, []
    for name, arr in arrays.items():
        arr = np.ascontiguousarray(arr)
        fed[f"in_{name}"] = arr
        aps.append(nc.dram_tensor(f"in_{name}", arr.shape, mybir.dt.from_np(arr.dtype), kind="ExternalInput").ap())
    aps.append(nc.dram_tensor("out_dram", _OUT, F32, kind="ExternalOutput").ap())
    build(nc, *aps)
    r = _run(nc, [fed], core_ids=[0])
    return r.results[0]["out_dram"]
```
